# Optimizing a Trainium2 kernel written in Bass

```python
import numpy as np
import jax
import jax.numpy as jnp

def _softmax(x, axis=-1):
    return jax.nn.softmax(x, axis=axis)
def _gelu(x):
    return jax.nn.gelu(x, approximate=True)
def _silu(x):
    return jax.nn.silu(x)
def _sigmoid(x):
    return jax.nn.sigmoid(x)
def _layernorm(x, axis=-1, eps=1e-5):
    m = jnp.mean(x, axis=axis, keepdims=True)
    v = jnp.var(x, axis=axis, keepdims=True)
    return (x - m) / jnp.sqrt(v + eps)
def _scatter_add(tgt, idx, src, axis=0):
    return tgt.at[idx].add(src)
def _segment_sum(src, seg, n):
    return jax.ops.segment_sum(src, seg, n)

kernel_name = 'mk_conv_seq_d2_conv_nchw512_09a131'

def setup_inputs(seed: int = 0):
    np.random.seed(seed)
    _w = jnp.asarray
    def _rec_inputs():
        import jax
        import jax.numpy as jnp
        _gk = jax.random.key(seed)
        x = -0.0002928 + 1 * jax.random.normal(jax.random.fold_in(_gk, 1), (8, 512, 32, 32), jnp.float32)
        return x
    x = _rec_inputs()
    def _L0_conv_setup():
        import math
        import jax, jax.numpy as jnp
        import numpy as np
        NUM_HEADS = 8
        GROUPS = 32
        EPS = 1e-05

        def group_norm(x, w, b):
            B, C, H, W = x.shape
            xg = x.reshape(B, GROUPS, C // GROUPS, H, W)
            mu = xg.mean(axis=(2, 3, 4), keepdims=True)
            var = xg.var(axis=(2, 3, 4), keepdims=True)
            xn = ((xg - mu) * jax.lax.rsqrt(var + EPS)).reshape(B, C, H, W)
            return xn * w[None, :, None, None] + b[None, :, None, None]
        key = jax.random.key(seed)
        ks = jax.random.split(key, 3)
        B, C, H, W = (8, 512, 32, 32)
        x = jax.random.normal(ks[0], (B, C, H, W), dtype=jnp.float32)
        norm_w = jnp.ones((C,), jnp.float32)
        norm_b = jnp.zeros((C,), jnp.float32)
        qkv_w = jax.random.normal(ks[1], (3 * C, C), dtype=jnp.float32) * (1.0 / math.sqrt(C))
        qkv_b = jnp.zeros((3 * C,), jnp.float32)
        proj_w = jax.random.normal(ks[2], (C, C), dtype=jnp.float32) * (1.0 / math.sqrt(C))
        proj_b = jnp.zeros((C,), jnp.float32)
        return {'x': x, 'norm_w': norm_w, 'norm_b': norm_b, 'qkv_w': qkv_w, 'qkv_b': qkv_b, 'proj_w': proj_w, 'proj_b': proj_b}
    _L0_conv_all = _L0_conv_setup()
    _L0_conv_in = {k: v for k, v in _L0_conv_all.items() if k in ('norm_w', 'norm_b', 'qkv_w', 'qkv_b', 'proj_w', 'proj_b', )}
    del _L0_conv_all

    def _L1_conv_setup():
        import jax, jax.numpy as jnp
        import numpy as np
        C = 512
        HEADS = 8
        HEAD_DIM = C // HEADS
        GROUPS = 32
        EPS = 1e-05

        def group_norm(x, scale, bias):
            b, c, h, w = x.shape
            xg = x.reshape(b, GROUPS, -1)
            mean = xg.mean(axis=-1, keepdims=True)
            var = xg.var(axis=-1, keepdims=True)
            xg = (xg - mean) * jax.lax.rsqrt(var + EPS)
            x = xg.reshape(b, c, h, w)
            return x * scale[None, :, None, None] + bias[None, :, None, None]

        def conv1x1(x, w, b):
            return jnp.einsum('oc,bchw->bohw', w, x) + b[None, :, None, None]
        key = jax.random.key(seed)
        ks = jax.random.split(key, 11)
        s = 1.0 / np.sqrt(C)
        return {'x': jax.random.normal(ks[0], (8, C, 32, 32), jnp.float32), 'gn_scale': jnp.ones((C,), jnp.float32), 'gn_bias': jnp.zeros((C,), jnp.float32), 'wq': jax.random.normal(ks[1], (C, C), jnp.float32) * s, 'bq': jax.random.normal(ks[2], (C,), jnp.float32) * 0.01, 'wk': jax.random.normal(ks[3], (C, C), jnp.float32) * s, 'bk': jax.random.normal(ks[4], (C,), jnp.float32) * 0.01, 'wv': jax.random.normal(ks[5], (C, C), jnp.float32) * s, 'bv': jax.random.normal(ks[6], (C,), jnp.float32) * 0.01, 'wp': jax.random.normal(ks[7], (C, C), jnp.float32) * s, 'bp': jax.random.normal(ks[8], (C,), jnp.float32) * 0.01}
    _L1_conv_all = _L1_conv_setup()
    _L1_conv_in = {k: v for k, v in _L1_conv_all.items() if k in ('gn_scale', 'gn_bias', 'wq', 'bq', 'wk', 'bk', 'wv', 'bv', 'wp', 'bp', )}
    del _L1_conv_all

    return {
        "x": x,
        "L0_conv_norm_w": _L0_conv_in["norm_w"],
        "L0_conv_norm_b": _L0_conv_in["norm_b"],
        "L0_conv_qkv_w": _L0_conv_in["qkv_w"],
        "L0_conv_qkv_b": _L0_conv_in["qkv_b"],
        "L0_conv_proj_w": _L0_conv_in["proj_w"],
        "L0_conv_proj_b": _L0_conv_in["proj_b"],
        "L1_conv_gn_scale": _L1_conv_in["gn_scale"],
        "L1_conv_gn_bias": _L1_conv_in["gn_bias"],
        "L1_conv_wq": _L1_conv_in["wq"],
        "L1_conv_bq": _L1_conv_in["bq"],
        "L1_conv_wk": _L1_conv_in["wk"],
        "L1_conv_bk": _L1_conv_in["bk"],
        "L1_conv_wv": _L1_conv_in["wv"],
        "L1_conv_bv": _L1_conv_in["bv"],
        "L1_conv_wp": _L1_conv_in["wp"],
        "L1_conv_bp": _L1_conv_in["bp"],
    }

def reference(x, L0_conv_norm_w, L0_conv_norm_b, L0_conv_qkv_w, L0_conv_qkv_b, L0_conv_proj_w, L0_conv_proj_b, L1_conv_gn_scale, L1_conv_gn_bias, L1_conv_wq, L1_conv_bq, L1_conv_wk, L1_conv_bk, L1_conv_wv, L1_conv_bv, L1_conv_wp, L1_conv_bp):
    import jax
    import jax.numpy as jnp
    def _L0_conv_ref(x, norm_w, norm_b, qkv_w, qkv_b, proj_w, proj_b):
        import math
        import jax, jax.numpy as jnp
        import numpy as np
        NUM_HEADS = 8
        GROUPS = 32
        EPS = 1e-05

        def group_norm(x, w, b):
            B, C, H, W = x.shape
            xg = x.reshape(B, GROUPS, C // GROUPS, H, W)
            mu = xg.mean(axis=(2, 3, 4), keepdims=True)
            var = xg.var(axis=(2, 3, 4), keepdims=True)
            xn = ((xg - mu) * jax.lax.rsqrt(var + EPS)).reshape(B, C, H, W)
            return xn * w[None, :, None, None] + b[None, :, None, None]
        B, C, H, W = x.shape
        T = H * W
        heads = NUM_HEADS
        ch = C // heads
        xn = group_norm(x, norm_w, norm_b)
        qkv = jnp.einsum('oc,bchw->bohw', qkv_w, xn).reshape(B, 3 * C, T) + qkv_b[None, :, None]
        qkv = qkv.reshape(B * heads, 3 * ch, T)
        q, k, v = jnp.split(qkv, 3, axis=1)
        scale = 1.0 / math.sqrt(math.sqrt(ch))
        w = jnp.einsum('bct,bcs->bts', q * scale, k * scale)
        w = jax.nn.softmax(w.astype(jnp.float32), axis=-1).astype(qkv.dtype)
        a = jnp.einsum('bts,bcs->bct', w, v)
        h = a.reshape(B, C, H, W)
        h = jnp.einsum('oc,bchw->bohw', proj_w, h) + proj_b[None, :, None, None]
        return x + h

    def _L1_conv_ref(x, gn_scale, gn_bias, wq, bq, wk, bk, wv, bv, wp, bp):
        import jax, jax.numpy as jnp
        import numpy as np
        C = 512
        HEADS = 8
        HEAD_DIM = C // HEADS
        GROUPS = 32
        EPS = 1e-05

        def group_norm(x, scale, bias):
            b, c, h, w = x.shape
            xg = x.reshape(b, GROUPS, -1)
            mean = xg.mean(axis=-1, keepdims=True)
            var = xg.var(axis=-1, keepdims=True)
            xg = (xg - mean) * jax.lax.rsqrt(var + EPS)
            x = xg.reshape(b, c, h, w)
            return x * scale[None, :, None, None] + bias[None, :, None, None]

        def conv1x1(x, w, b):
            return jnp.einsum('oc,bchw->bohw', w, x) + b[None, :, None, None]
        b, c, h, w = x.shape
        n = h * w
        h_in = x
        xn = group_norm(x, gn_scale, gn_bias)
        q = conv1x1(xn, wq, bq).reshape(b, HEADS, HEAD_DIM, n)
        k = conv1x1(xn, wk, bk).reshape(b, HEADS, HEAD_DIM, n)
        v = conv1x1(xn, wv, bv).reshape(b, HEADS, HEAD_DIM, n)
        scale = 1.0 / np.sqrt(HEAD_DIM).astype(np.float32)
        attn = jnp.einsum('bhcn,bhcm->bhnm', q, k) * scale
        attn = jax.nn.softmax(attn, axis=-1)
        out = jnp.einsum('bhnm,bhcm->bhcn', attn, v)
        out = out.reshape(b, c, h, w)
        out = conv1x1(out, wp, bp)
        return out + h_in

    def _gn(v, G=32, eps=1e-5):
        B_, C_, H_, W_ = v.shape
        g = v.reshape(B_, G, C_ // G, H_, W_)
        m = jnp.mean(g, axis=(2, 3, 4), keepdims=True)
        s = jnp.var(g, axis=(2, 3, 4), keepdims=True)
        return ((g - m) / jnp.sqrt(s + eps)).reshape(v.shape)

    def _ln_c(v, eps=1e-6):
        m = jnp.mean(v, axis=1, keepdims=True)
        s = jnp.var(v, axis=1, keepdims=True)
        return (v - m) / jnp.sqrt(s + eps)

    def _ln_t(v, eps=1e-5):
        m = jnp.mean(v, axis=-1, keepdims=True)
        s = jnp.var(v, axis=-1, keepdims=True)
        return (v - m) / jnp.sqrt(s + eps)

    def _to_tokens(v):
        B_, C_, H_, W_ = v.shape
        return v.reshape(B_, C_, H_ * W_).transpose(0, 2, 1)
    def _from_tokens(t, like):
        B_, C_, H_, W_ = like.shape
        return t.transpose(0, 2, 1).reshape(B_, C_, H_, W_)

    x = _L0_conv_ref(x, L0_conv_norm_w, L0_conv_norm_b, L0_conv_qkv_w, L0_conv_qkv_b, L0_conv_proj_w, L0_conv_proj_b)
    x = _L1_conv_ref(x, L1_conv_gn_scale, L1_conv_gn_bias, L1_conv_wq, L1_conv_bq, L1_conv_wk, L1_conv_bk, L1_conv_wv, L1_conv_bv, L1_conv_wp, L1_conv_bp)
    return x


_drawn_inputs = setup_inputs


def setup_inputs(seed=0):
    import zlib

    import numpy as np

    out = dict(_drawn_inputs(seed))
    spreads = {'L0_conv_norm_w': (1.0, 0.2),
     'L0_conv_norm_b': (0.0, 0.1),
     'L0_conv_qkv_b': (0.0, 0.1),
     'L0_conv_proj_b': (0.0, 0.1),
     'L1_conv_gn_scale': (1.0, 0.2),
     'L1_conv_gn_bias': (0.0, 0.1)}
    factors = {'L1_conv_bq': 64.0, 'L1_conv_bk': 64.0, 'L1_conv_bv': 5.739, 'L1_conv_bp': 6.169}
    for name, (base, spread) in spreads.items():
        noise = np.random.default_rng([zlib.crc32(name.encode()), seed]).standard_normal(out[name].shape)
        drawn = base * np.exp(spread * noise) if base else spread * noise
        out[name] = jnp.asarray(drawn.astype(out[name].dtype))
    for name, factor in factors.items():
        out[name] = (out[name] * factor).astype(out[name].dtype)
    return out
```

```python
from contextlib import ExitStack

import concourse.bass as bass
from concourse import mybir

F32 = mybir.dt.float32
F32R = mybir.dt.float32r
ALU = mybir.AluOpType
ACT = mybir.ActivationFunctionType
AX = mybir.AxisListType

P = 128
LAYERS, B, C, T = 2, 8, 512, 1024
N = LAYERS * B
HEADS, CH = 8, 64
GROUP = 16
CT = C // P
QT = T // P
G = HEADS * QT
LAG = 3
HALF = 512
NG = G // 4
NP = 2 * CT
KSCALE = 1.0 / 8.0
EPS = 1e-5
UNITS = HEADS + 2 * CT
CHUNKS = UNITS // 2
RES = 3
RES_PER = [len(range(s, NP, RES)) for s in range(RES)]
QK_PIECES = {0: (0, 0, 6), 1: (0, 6, 12), 3: (1, 0, 4), 4: (1, 4, 8), 5: (1, 8, 12)}
TERMS = ((0, 0), (0, 1), (1, 0))


def attention_blocks(nc, x, weights, params, gn_params, consts, hidden, split, out):
    ctx = ExitStack()
    with ctx:
        def sb(name, shape, dt=F32):
            return ctx.enter_context(nc.sbuf_tensor(name, shape, dt))

        def sem(name):
            return ctx.enter_context(nc.semaphore(name))

        wqk = sb("wqk", [P, HEADS, 2, CT, P], F32R)
        wvp = sb("wvp", [P, CT, 2, HALF], F32R)
        xin = sb("xin", [P, 2, T])
        xn = sb("xn", [P, 2, CT, T], F32R)
        va = sb("va", [P, CT + 1, 2 * T], F32R)
        q_hl = sb("q_hl", [P, 2, T], F32R)
        q_lh = sb("q_lh", [P, 2, T], F32R)
        k_lh = sb("k_lh", [P, 2, T], F32R)
        probs = sb("probs", [P, LAG, T])
        probs_t = sb("probs_t", [P, 2, QT, HALF], F32R)
        head_out = sb("head_out", [P, HALF])
        res = sb("res", [P, RES, HALF])
        cst = sb("cst", [P, 2, P])
        par = sb("par", [P, 20])
        qk_bias = sb("qk_bias", [P, HEADS])
        k_scale = sb("k_scale", [P, 1])
        gn_par = sb("gn_par", [P, 2 * CT])
        neg_max = sb("neg_max", [P, 4])
        row_sum = sb("row_sum", [P, 4])
        row_inv = sb("row_inv", [P, 4])
        bn_part = sb("bn_part", [P, 2, 2, 6])
        bn_mv = sb("bn_mv", [P, 2, 2])
        g_mean = sb("g_mean", [P, 2])
        g_dev = sb("g_dev", [P, 2])
        g_sq = sb("g_sq", [P, 2])
        g_spread = sb("g_spread", [P, 2])
        g_var = sb("g_var", [P, 2])
        minus_half = sb("minus_half", [P, 2])
        g_rstd = sb("g_rstd", [P, 2])
        g_scale = sb("g_scale", [P, 2])
        g_ms = sb("g_ms", [P, 2])
        g_shift = sb("g_shift", [P, 2])
        ident = cst[:, 0, :]
        gmat = cst[:, 1, :]

        ps_s = ctx.enter_context(nc.psum_tensor("ps_s", [P, 4, HALF], F32))
        ps_t = ctx.enter_context(nc.psum_tensor("ps_t", [P, 2, HALF], F32))
        ps_pv = ctx.enter_context(nc.psum_tensor("ps_pv", [P, HALF], F32))
        ps_qk = ctx.enter_context(nc.psum_tensor("ps_qk", [P, HALF], F32))

        v_view = va[:, 1:CT + 1, :].rearrange("p r (h t c) -> p (r h) t c", h=2, t=QT)
        a_view = va[:, 0:CT, :].rearrange("p r (w t) -> p r w t", w=2)

        s_const = sem("s_const")
        s_par = sem("s_par")
        s_gnpar = sem("s_gnpar")
        s_kscale = sem("s_kscale")
        s_qkbias = sem("s_qkbias")
        s_chunk = [sem("s_chunk0"), sem("s_chunk1")]
        s_kscaled = sem("s_kscaled")
        s_whigh = sem("s_whigh")
        s_wlow = sem("s_wlow")
        s_wstored = [sem("s_wstored0"), sem("s_wstored1")]
        s_wqk = sem("s_wqk")
        s_wvp = [sem(f"s_wvp{i}") for i in range(CT)]
        s_x = sem("s_x")
        s_stats = sem("s_stats")
        s_gmean = sem("s_gmean")
        s_spread = sem("s_spread")
        s_gspread = sem("s_gspread")
        s_gvar = sem("s_gvar")
        s_shift = sem("s_shift")
        s_applied = sem("s_applied")
        s_xhigh = sem("s_xhigh")
        s_xlow = sem("s_xlow")
        s_dve = sem("s_dve")
        s_pool = sem("s_pool")
        s_qk = sem("s_qk")
        s_qkhigh = sem("s_qkhigh")
        s_qklow = sem("s_qklow")
        s_swap = [sem("s_swap0"), sem("s_swap1")]
        s_v = sem("s_v")
        s_vhigh = sem("s_vhigh")
        s_vlow = sem("s_vlow")
        s_score = sem("s_score")
        s_max = sem("s_max")
        s_exp = sem("s_exp")
        s_inv = sem("s_inv")
        s_norm = sem("s_norm")
        s_trans = sem("s_trans")
        s_phigh = sem("s_phigh")
        s_plow = sem("s_plow")
        s_pv = sem("s_pv")
        s_olow = sem("s_olow")
        s_osum = sem("s_osum")
        s_ohigh = sem("s_ohigh")
        s_o = sem("s_o")
        s_proj = sem("s_proj")
        s_y = sem("s_y")
        s_res = [sem(f"s_res{i}") for i in range(RES)]
        s_out = [sem(f"s_out{i}") for i in range(RES)]

        def image(t, b):
            return t[b].rearrange("(ct p) n -> p ct n", p=P)

        def wait_apart(eng, *waits):
            for _, value in waits:
                if not isinstance(value, int):
                    eng.compute_val(value)
            eng.wait_ge(s_const, 16)
            for semaphore, value in waits:
                eng.wait_ge(semaphore, value)

        block = ctx.enter_context(nc.Block())

        @block.sync
        def _(sp):
            def swap_q(n, h):
                sp.wait_ge(s_qklow, 16 * n + 2 * h + 2)
                s = h % 2
                sp.dma_start(q_lh[0:CH, s, :].bitcast(F32), q_hl[CH:P, s, :].bitcast(F32)).then_inc(s_swap[s], 16)
                sp.dma_start(q_lh[CH:P, s, :].bitcast(F32), q_hl[0:CH, s, :].bitcast(F32)).then_inc(s_swap[s], 16)

            def load_x(pair, m, x_free):
                dst = xin[:, :, :]
                wait_apart(sp, (s_xlow, x_free))
                with sp.If(m < B):
                    sp.dma_start(dst, image(x, m % B)[:, 2 * pair:2 * pair + 2, :]).then_inc(s_x, 16)
                with sp.Else():
                    sp.dma_start(dst, image(hidden, m % B)[:, 2 * pair:2 * pair + 2, :]).then_inc(s_x, 16)

            def load_unit(dst, layer, unit, s):
                sp.dma_start(dst, split[layer, unit]).then_inc(s, 16)

            sp.dma_start(xin[:, :, :], image(x, 0)[:, 0:2, :]).then_inc(s_x, 16)
            sp.dma_start(gn_par[:, :], gn_params[0]).then_inc(s_gnpar, 16)
            sp.dma_start(par[:, :], params[0]).then_inc(s_par, 16)
            sp.dma_start(cst[:, :, :], consts).then_inc(s_const, 16)
            with sp.Fori(0, LAYERS) as l:
                for c in range(2):
                    sp.dma_start(probs[:, c, :], weights[l, c]).then_inc(s_chunk[c], 16)
                for c in range(CHUNKS):
                    sp.wait_ge(s_wlow, CHUNKS * l + c + 1)
                    for w in range(2):
                        sp.dma_start(split[l, 2 * c:2 * c + 2, :, w * HALF:(w + 1) * HALF].rearrange("u p n -> p u n"),
                                     probs_t[:, w, 2 * (c % 2):2 * (c % 2) + 2, :].bitcast(F32))\
                            .then_inc(s_wstored[c % 2], 16)
                    if c + 2 < CHUNKS:
                        sp.dma_start(probs[:, c % 2, :], weights[l, c + 2]).then_inc(s_chunk[c % 2], 16)
                wait_apart(sp, *((s_wstored[s], 16 * CHUNKS * (l + 1)) for s in range(2)))
            for h in range(HEADS):
                load_unit(wqk[:, h].rearrange("p w c n -> p (w c n)").bitcast(F32), 0, h, s_wqk)
            for ct in range(CT):
                load_unit(wvp[:, ct].rearrange("p w n -> p (w n)").bitcast(F32), 0, HEADS + ct, s_wvp[ct])
            sp.wait_ge(s_xlow, 2)
            sp.dma_start(xin[:, :, :], image(x, 0)[:, 2:4, :]).then_inc(s_x, 16)

            with sp.Fori(0, N) as n:
                layer = n // B
                swap_q(n, 0)
                sp.wait_ge(s_v, QT * n + QT)
                for o in range(CT):
                    load_unit(wvp[:, o].rearrange("p w n -> p (w n)").bitcast(F32), layer, HEADS + CT + o, s_wvp[o])
                sp.wait_ge(s_xlow, CT * n + CT)
                nxt = (n + 1) // B % LAYERS
                sp.dma_start(gn_par[:, :], gn_params[nxt]).then_inc(s_gnpar, 16)
                load_x(0, n + 1, CT * n + CT)

                def load_res(j):
                    o, k, s = j % CT, j // CT, j % RES
                    src = slice(k * HALF, (k + 1) * HALF)
                    if j >= RES:
                        wait_apart(sp, (s_out[s], 16 * (RES_PER[s] * n + j // RES)))
                    with sp.If(n < B):
                        sp.dma_start(res[:, s, :], image(x, n % B)[:, o, src]).then_inc(s_res[s], 16)
                    with sp.Else():
                        sp.dma_start(res[:, s, :], image(hidden, n % B)[:, o, src]).then_inc(s_res[s], 16)

                def store_res(j):
                    o, k, s = j % CT, j // CT, j % RES
                    dst = slice(k * HALF, (k + 1) * HALF)
                    wait_apart(sp, (s_y, NP * n + j + 1))
                    with sp.If(n < B):
                        sp.dma_start(image(hidden, n % B)[:, o, dst], res[:, s, :]).then_inc(s_out[s], 16)
                    with sp.Else():
                        sp.dma_start(image(out, n % B)[:, o, dst], res[:, s, :]).then_inc(s_out[s], 16)

                for h in range(1, HEADS):
                    swap_q(n, h)
                    if h == 1:
                        for j in range(RES):
                            load_res(j)
                wait_apart(sp, (s_qk, 2 * HEADS * n + 2 * HEADS))
                with sp.If(n % B == B - 1):
                    for h in range(HEADS):
                        load_unit(wqk[:, h].rearrange("p w c n -> p (w c n)").bitcast(F32), nxt, h, s_wqk)
                load_x(1, n + 1, CT * n + CT + 2)
                for j in range(NP):
                    store_res(j)
                    if j >= CT:
                        ct = j - CT
                        load_unit(wvp[:, ct].rearrange("p w n -> p (w n)").bitcast(F32), nxt, HEADS + ct, s_wvp[ct])
                    if 1 <= j and j + 2 < NP:
                        load_res(j + 2)
                sp.dma_start(par[:, :], params[nxt]).then_inc(s_par, 16)
                wait_apart(sp, *((s_out[s], 16 * RES_PER[s] * (n + 1)) for s in range(RES)))
            sp.wait_ge(s_par, 16 * (N + 1))
            sp.wait_ge(s_wqk, 16 * HEADS * (LAYERS + 1))
            for ct in range(CT):
                sp.wait_ge(s_wvp[ct], 16 * (2 * N + 1))
            sp.wait_ge(s_x, 16 * 2 * (N + 1))

        @block.gpsimd
        def _(pool):
            PER_GN = 6

            def gn_coeffs(m, pair):
                base = PER_GN * m
                c = 3 * pair
                w = gn_par[:, 2 * pair:2 * pair + 2]
                b = gn_par[:, CT + 2 * pair:CT + 2 * pair + 2]
                pool.wait_ge(s_gnpar, 16 * m + 16)
                pool.wait_ge(s_gvar, 2 * m + pair + 1)
                nc.gpsimd.tensor_tensor(g_rstd[:, :], g_var[:, :], minus_half[:, :], ALU.pow).then_inc(s_pool, 1)
                pool.wait_ge(s_pool, base + c + 1)
                nc.gpsimd.tensor_tensor(g_scale[:, :], g_rstd[:, :], w, ALU.mult).then_inc(s_pool, 1)
                pool.wait_ge(s_pool, base + c + 2)
                nc.gpsimd.tensor_tensor(g_ms[:, :], g_mean[:, :], g_scale[:, :], ALU.mult).then_inc(s_pool, 1)
                pool.wait_ge(s_pool, base + c + 3)
                nc.gpsimd.tensor_tensor(g_shift[:, :], b, g_ms[:, :], ALU.subtract).then_inc(s_shift, 1)
                wait_apart(pool, (s_shift, 2 * m + pair + 1))
                for i in range(2):
                    nc.gpsimd.tensor_scalar(xin[:, i, :], xin[:, i, :], g_scale[:, i:i + 1], g_shift[:, i:i + 1],
                                            ALU.mult, ALU.add).then_inc(s_applied, 1)

            def gn_low(m, pair, i):
                ct = 2 * pair + i
                pool.wait_ge(s_xhigh, CT * m + ct + 1)
                nc.gpsimd.tensor_tensor(xn[:, 1, ct, :], xin[:, i, :], xn[:, 0, ct, :].bitcast(F32),
                                        ALU.subtract).then_inc(s_xlow, 1)

            pool.wait_ge(s_kscale, 3)
            with pool.Fori(0, LAYERS) as l:
                for c in range(HEADS // 2):
                    wait_apart(pool, (s_chunk[c % 2], 16 * (CHUNKS // 2 * l + c // 2 + 1)))
                    k_part = probs[:, c % 2, :].rearrange("p (u n) -> p u n", n=P)[:, :, CH:P]
                    nc.gpsimd.tensor_scalar(k_part, k_part, KSCALE, 1.0, ALU.mult, ALU.mult).then_inc(s_kscaled, 1)
            for pair in range(2):
                gn_coeffs(0, pair)
                for i in range(2):
                    gn_low(0, pair, i)

            with pool.Fori(0, N) as n:
                wait_apart(pool, (s_par, 16 * n + 16))
                nc.gpsimd.tensor_scalar(qk_bias[:, :], par[:, 0:HEADS], k_scale[:, 0:1], 1.0,
                                        ALU.mult, ALU.mult).then_inc(s_qkbias, 1)

                def normalise(g):
                    s = g % LAG
                    wait_apart(pool, (s_inv, G * n + g + 1))
                    nc.gpsimd.tensor_scalar(probs[:, s, :], probs[:, s, :], row_inv[:, g % 4:g % 4 + 1], 1.0,
                                            ALU.mult, ALU.mult).then_inc(s_norm, 1)

                def split_out(k, before, count):
                    h = k // 2
                    r = slice(CH * (h % 2), CH * (h % 2) + CH)
                    cols = slice(HALF * (k % 2), HALF * (k % 2) + HALF)
                    wait_apart(pool, (before, count), (s_osum, NG * n + k + 1))
                    nc.gpsimd.tensor_scalar(a_view[r, h // 2, 0, cols], head_out[r, :], 1.0, 1.0,
                                            ALU.mult, ALU.mult).then_inc(s_ohigh, 1)
                    pool.wait_ge(s_ohigh, NG * n + k + 1)
                    nc.gpsimd.tensor_tensor(a_view[r, h // 2, 1, cols], head_out[r, :],
                                            a_view[r, h // 2, 0, cols].bitcast(F32), ALU.subtract).then_inc(s_o, 1)
                    pool.wait_ge(s_o, NG * n + k + 1)

                for g in range(G + LAG):
                    if 1 <= g <= G:
                        normalise(g - 1)
                    if g >= 7 and g % 4 == 3:
                        split_out((g - 7) // 4, s_norm, G * n + g)
                    if g == 57:
                        gn_coeffs(n + 1, 0)
                    if g in (59, 60):
                        gn_low(n + 1, 0, g - 59)
                    if g == 64:
                        gn_coeffs(n + 1, 1)
                    if g in (65, 66):
                        gn_low(n + 1, 1, g - 65)
                split_out(NG - 1, s_xlow, CT * n + 2 * CT)

        @block.scalar
        def _(act):
            def gn_high(m, ct):
                act.wait_ge(s_applied, CT * m + ct + 1)
                nc.scalar.activation(xn[:, 0, ct, :], xin[:, ct % 2, :], ACT.Copy).then_inc(s_xhigh, 1)

            with act.Fori(0, LAYERS) as l:
                for c in range(CHUNKS):
                    s = c % 2
                    act.wait_ge(s_chunk[s], 16 * (CHUNKS // 2 * l + c // 2 + 1))
                    if c < HEADS // 2:
                        act.wait_ge(s_kscaled, HEADS // 2 * l + c + 1)
                    if c >= 2:
                        act.wait_ge(s_wstored[s], 32 * (CHUNKS // 2 * l + c // 2))
                    nc.scalar.activation(probs_t[:, 0, 2 * s:2 * s + 2, :],
                                         probs[:, s, :].rearrange("p (u n) -> p u n", u=2), ACT.Copy).then_inc(s_whigh, 1)
            for ct in range(CT):
                gn_high(0, ct)

            with act.Fori(0, N) as n:
                def qk_high(i):
                    h, k = i // 2, i % 2
                    cols = slice(HALF * k, HALF * k + HALF)
                    act.wait_ge(s_qk, 16 * n + i + 1)
                    if i == 0:
                        act.wait_ge(s_qkbias, n + 1)
                    nc.scalar.activation(q_hl[0:CH, h % 2, cols], ps_qk[0:CH, :], ACT.Identity,
                                         bias=qk_bias[0:CH, h:h + 1])
                    nc.scalar.activation(k_lh[CH:P, h % 2, cols], ps_qk[CH:P, :], ACT.Identity,
                                         bias=qk_bias[CH:P, h:h + 1]).then_inc(s_qkhigh, 1)

                def v_high(t):
                    act.wait_ge(s_v, QT * n + t + 1)
                    nc.scalar.activation(v_view[:, :, t, 0:CH], ps_s[:, t % 4, :].rearrange("p (h c) -> p h c", h=HEADS),
                                         ACT.Copy).then_inc(s_vhigh, 1)

                def exp(g):
                    b = 2 * (g % 2)
                    act.wait_ge(s_max, G * n + g + 1)
                    nc.scalar.activation(probs[:, g % LAG, :].rearrange("p (b n) -> p b n", b=2), ps_s[:, b:b + 2, :],
                                         ACT.Exp, bias=neg_max[:, g % 4:g % 4 + 1],
                                         accum_out=row_sum[:, g % 4:g % 4 + 1]).then_inc(s_exp, 1)

                def probs_high(g, b):
                    act.wait_ge(s_trans, 2 * G * n + 2 * g + b + 1)
                    if g % 4 == 0 and b == 0 and g:
                        act.wait_ge(s_pv, NG * n + g // 4)
                    q = P * (g % 4)
                    nc.scalar.activation(probs_t[:, 0, 4 * b:4 * b + 4, q:q + P],
                                         ps_t[:, b, :].rearrange("p (k q) -> p k q", k=4), ACT.Copy).then_inc(s_phigh, 1)

                def out_low_half(k):
                    act.wait_ge(s_pv, NG * n + k + 1)
                    if k:
                        act.wait_ge(s_o, NG * n + k)
                    nc.scalar.activation(head_out[0:CH, :], ps_pv[CH:P, :], ACT.Copy).then_inc(s_olow, 1)

                qk_high(0)
                v_high(0)
                v_high(1)
                qk_high(1)
                for t in range(2, QT):
                    v_high(t)
                for g in range(G + LAG):
                    qt = g % QT
                    if g >= 7 and g % 4 == 3:
                        out_low_half((g - 7) // 4)
                    if g >= LAG:
                        probs_high(g - LAG, 0)
                        probs_high(g - LAG, 1)
                    if 1 <= g <= G:
                        exp(g - 1)
                    if g < G - QT and qt == 2:
                        qk_high(2 * (g // QT + 1))
                    if g < G - QT and qt == 6:
                        qk_high(2 * (g // QT + 1) + 1)
                    if g in (58, 59):
                        gn_high(n + 1, g - 58)
                    if g == 65:
                        gn_high(n + 1, 2)
                        gn_high(n + 1, 3)
                out_low_half(NG - 1)

        @block.vector
        def _(dve):
            PER_GN = 8
            nc.vector.memset(minus_half[:, :], -0.5).then_inc(s_kscale, 1)
            nc.vector.memset(k_scale[0:CH, :], 1.0).then_inc(s_kscale, 1)
            nc.vector.memset(k_scale[CH:P, :], KSCALE).then_inc(s_kscale, 1)

            def gn_stats(m, pair):
                c = PER_GN * m + 4 * pair
                dve.wait_ge(s_x, 16 * (2 * m + pair + 1))
                for i in range(2):
                    for k in range(2):
                        last = nc.vector.bn_stats(bn_part[:, i, k, :], xin[:, i, HALF * k:HALF * k + HALF])
                last.then_inc(s_dve, 1)
                wait_apart(dve, (s_dve, c + 1))
                for i in range(2):
                    last = nc.vector.bn_aggr(bn_mv[:, i, :], bn_part[:, i, :, :].rearrange("p k s -> p (k s)"))
                last.then_inc(s_stats, 1)

            def gn_spread(m, pair):
                c = PER_GN * m + 4 * pair
                dve.wait_ge(s_gmean, 2 * m + pair + 1)
                dve.wait_ge(s_stats, 2 * m + pair + 1)
                nc.vector.tensor_copy(g_mean[:, :], ps_qk[:, 0:2]).then_inc(s_dve, 1)
                dve.wait_ge(s_dve, c + 2)
                nc.vector.tensor_tensor(g_dev[:, :], bn_mv[:, :, 0], g_mean[:, :], ALU.subtract).then_inc(s_dve, 1)
                dve.wait_ge(s_dve, c + 3)
                nc.vector.tensor_tensor(g_sq[:, :], g_dev[:, :], g_dev[:, :], ALU.mult).then_inc(s_dve, 1)
                dve.wait_ge(s_dve, c + 4)
                nc.vector.tensor_tensor(g_spread[:, :], g_sq[:, :], bn_mv[:, :, 1], ALU.add).then_inc(s_spread, 1)

            def gn_var(m, pair):
                c = PER_GN * m + 4 * pair
                dve.wait_ge(s_gspread, 2 * m + pair + 1)
                nc.vector.tensor_scalar(g_var[:, :], ps_qk[:, 8:10], EPS, None, ALU.add).then_inc(s_gvar, 1)

            with dve.Fori(0, LAYERS) as l:
                for c in range(CHUNKS):
                    s = c % 2
                    dve.wait_ge(s_whigh, CHUNKS * l + c + 1)
                    src = probs[:, s, :].rearrange("p (u n) -> p u n", u=2)
                    nc.vector.tensor_tensor(probs_t[:, 1, 2 * s:2 * s + 2, :], src,
                                            probs_t[:, 0, 2 * s:2 * s + 2, :].bitcast(F32), ALU.subtract).then_inc(s_wlow, 1)
            for pair in range(2):
                gn_stats(0, pair)
                gn_spread(0, pair)
                gn_var(0, pair)

            with dve.Fori(0, N) as n:
                def qk_low(i):
                    h, k = i // 2, i % 2
                    cols = slice(HALF * k, HALF * k + HALF)
                    dve.wait_ge(s_qkhigh, 16 * n + i + 1)
                    nc.vector.scalar_tensor_tensor(q_hl[CH:P, h % 2, cols], ps_qk[0:CH, :], qk_bias[0:CH, h:h + 1],
                                                   q_hl[0:CH, h % 2, cols].bitcast(F32), ALU.add, ALU.subtract)
                    nc.vector.scalar_tensor_tensor(k_lh[0:CH, h % 2, cols], ps_qk[CH:P, :], qk_bias[CH:P, h:h + 1],
                                                   k_lh[CH:P, h % 2, cols].bitcast(F32),
                                                   ALU.add, ALU.subtract).then_inc(s_qklow, 1)

                def v_low(t):
                    dve.wait_ge(s_vhigh, QT * n + t + 1)
                    nc.vector.tensor_tensor(v_view[:, :, t, CH:P], ps_s[:, t % 4, :].rearrange("p (h c) -> p h c", h=HEADS),
                                            v_view[:, :, t, 0:CH].bitcast(F32), ALU.subtract).then_inc(s_vlow, 1)

                def row_max(g):
                    b = 2 * (g % 2)
                    dve.wait_ge(s_score, G * n + g + 1)
                    nc.vector.reduce_max(neg_max[:, g % 4:g % 4 + 1], ps_s[:, b:b + 2, :], AX.XY,
                                         negate=True).then_inc(s_max, 1)

                def row_inverse(g):
                    dve.wait_ge(s_exp, G * n + g + 1)
                    nc.vector.reciprocal(row_inv[:, g % 4:g % 4 + 1], row_sum[:, g % 4:g % 4 + 1]).then_inc(s_inv, 1)

                def probs_low(g, b):
                    dve.wait_ge(s_phigh, 2 * G * n + 2 * g + b + 1)
                    q = P * (g % 4)
                    nc.vector.tensor_tensor(probs_t[:, 1, 4 * b:4 * b + 4, q:q + P],
                                            ps_t[:, b, :].rearrange("p (k q) -> p k q", k=4),
                                            probs_t[:, 0, 4 * b:4 * b + 4, q:q + P].bitcast(F32),
                                            ALU.subtract).then_inc(s_plow, 1)

                def out_sum(k):
                    h = k // 2
                    r = slice(CH * (h % 2), CH * (h % 2) + CH)
                    dve.wait_ge(s_olow, NG * n + k + 1)
                    nc.vector.scalar_tensor_tensor(head_out[r, :], ps_pv[0:CH, :], par[0:CH, HEADS + h:HEADS + h + 1],
                                                   head_out[0:CH, :], ALU.add, ALU.add).then_inc(s_osum, 1)

                def add_residual(j):
                    o, s = j % CT, j % RES
                    dve.wait_ge(s_proj, NP * n + j + 1)
                    dve.wait_ge(s_res[s], 16 * (RES_PER[s] * n + j // RES + 1))
                    nc.vector.scalar_tensor_tensor(res[:, s, :], ps_s[:, j % 4, :], par[:, 2 * HEADS + o:2 * HEADS + o + 1],
                                                   res[:, s, :], ALU.add, ALU.add).then_inc(s_y, 1)

                qk_low(0)
                v_low(0)
                v_low(1)
                qk_low(1)
                for t in range(2, QT):
                    v_low(t)
                for g in range(G + LAG):
                    qt = g % QT
                    if g >= 7 and g % 4 == 3:
                        out_sum((g - 7) // 4)
                    if g == 56:
                        gn_spread(n + 1, 0)
                    if g == 57:
                        gn_var(n + 1, 0)
                    if g == 63:
                        gn_spread(n + 1, 1)
                    if g == 64:
                        gn_var(n + 1, 1)
                    if g >= LAG:
                        probs_low(g - LAG, 0)
                        probs_low(g - LAG, 1)
                    if g < G:
                        row_max(g)
                    if 1 <= g <= G:
                        row_inverse(g - 1)
                    if g < G - QT and qt == 2:
                        qk_low(2 * (g // QT + 1))
                    if g < G - QT and qt == 6:
                        qk_low(2 * (g // QT + 1) + 1)
                    if g == 50:
                        gn_stats(n + 1, 0)
                    if g == 61:
                        gn_stats(n + 1, 1)
                    if g > G:
                        add_residual(g - G - 1)
                add_residual(2)
                out_sum(NG - 1)
                for j in range(3, NP):
                    add_residual(j)

        @block.tensor
        def _(pe):
            def group_mean(m, pair):
                pe.wait_ge(s_stats, 2 * m + pair + 1)
                nc.tensor.matmul(ps_qk[:, 0:2], gmat, bn_mv[:, :, 0], start=True, stop=True).then_inc(s_gmean, 1)

            def group_spread(m, pair):
                pe.wait_ge(s_spread, 2 * m + pair + 1)
                nc.tensor.matmul(ps_qk[:, 8:10], gmat, g_spread[:, :], start=True, stop=True).then_inc(s_gspread, 1)

            pe.wait_ge(s_const, 16)
            for pair in range(2):
                if pair:
                    pe.wait_ge(s_gvar, pair)
                group_mean(0, pair)
                group_spread(0, pair)

            with pe.Fori(0, N) as n:
                def project_qk(i, lo, hi):
                    h, k = i // 2, i % 2
                    if lo == 0 and i > 0:
                        pe.wait_ge(s_qklow, 16 * n + i)
                    for j in range(lo, hi):
                        w, v = TERMS[j // CT]
                        last = nc.tensor.matmul(ps_qk[:, :], wqk[:, h, w, j % CT, :], xn[:, v, j % CT, HALF * k:HALF * k + HALF],
                                                start=j == 0, stop=j == 3 * CT - 1)
                    if hi == 3 * CT:
                        last.then_inc(s_qk, 1)

                def project_v(t):
                    if t == 0:
                        pe.wait_ge(s_par, 16 * n + 16)
                    if t >= 4:
                        pe.wait_ge(s_vlow, QT * n + t - 3)
                    if t == 0:
                        for ct in range(CT):
                            pe.wait_ge(s_wvp[ct], 16 * (2 * n + 1))
                    for j in range(3 * CT):
                        w, v = TERMS[j // CT]
                        last = nc.tensor.matmul(ps_s[:, t % 4, :], xn[:, v, j % CT, P * t:P * t + P], wvp[:, j % CT, w, :],
                                                start=j == 0, stop=j == 3 * CT - 1)
                    last.then_inc(s_v, 1)

                def scores(g):
                    h, qt, b = g // QT, g % QT, 2 * (g % 2)
                    s = h % 2
                    if qt == 0:
                        pe.wait_ge(s_qklow, 16 * n + 2 * h + 2)
                        pe.wait_ge(s_swap[s], 32 * (HEADS // 2 * n + h // 2 + 1))
                    if g < 2:
                        pe.wait_ge(s_vlow, QT * n + 6 + 2 * g)
                    else:
                        pe.wait_ge(s_exp, G * n + g - 1)
                    for q, first in ((q_hl, True), (q_lh, False)):
                        for k in range(2):
                            last = nc.tensor.matmul(ps_s[:, b + k, :], q[:, s, P * qt:P * qt + P],
                                                    k_lh[:, s, HALF * k:HALF * k + HALF], start=first, stop=not first)
                    last.then_inc(s_score, 1)

                def transpose(g):
                    pe.wait_ge(s_norm, G * n + g + 1)
                    for b in range(2):
                        if g:
                            pe.wait_ge(s_plow, 2 * G * n + 2 * g + b - 1)
                        for k in range(4):
                            c = 4 * b + k
                            last = nc.tensor.transpose(ps_t[:, b, P * k:P * k + P], probs[:, g % LAG, P * c:P * c + P], ident)
                        last.then_inc(s_trans, 1)

                def probs_v(k):
                    h = k // 2
                    if k == 0:
                        pe.wait_ge(s_vlow, QT * n + QT)
                    pe.wait_ge(s_plow, 2 * G * n + 8 * k + 8)
                    if k:
                        pe.wait_ge(s_osum, NG * n + k)
                    for kt in range(QT):
                        for w in range(2):
                            last = nc.tensor.matmul(ps_pv[:, :], v_view[:, h, kt, :], probs_t[:, w, kt, :],
                                                    start=kt == 0 and w == 0, stop=kt == QT - 1 and w == 1)
                    last.then_inc(s_pv, 1)

                def project_out(j):
                    o, k = j % CT, j // CT
                    if j < 4:
                        if j in (0, 2):
                            pe.wait_ge(s_exp, G * n + G - 1 + j // 2)
                        pe.wait_ge(s_wvp[o], 16 * (2 * n + 2))
                    else:
                        pe.wait_ge(s_y, NP * n + j - 3)
                    pe.wait_ge(s_o, NG * n + NG - 1 + k)
                    for i in range(3 * CT):
                        w, v = TERMS[i // CT]
                        ct = i % CT
                        last = nc.tensor.matmul(ps_s[:, j % 4, :], wvp[:, o, w, P * ct:P * ct + P],
                                                a_view[:, ct, v, HALF * k:HALF * k + HALF], start=i == 0, stop=i == 3 * CT - 1)
                    last.then_inc(s_proj, 1)

                pe.wait_ge(s_xlow, CT * n + CT)
                pe.wait_ge(s_wqk, 16 * HEADS * (n // B + 1))
                project_qk(0, 0, 3 * CT)
                project_v(0)
                project_v(1)
                project_qk(1, 0, 3 * CT)
                for t in range(2, QT):
                    project_v(t)
                for g in range(G + LAG):
                    qt, h = g % QT, g // QT
                    if g >= LAG:
                        transpose(g - LAG)
                    if g < G:
                        scores(g)
                    if h < HEADS - 1 and qt in QK_PIECES:
                        k, lo, hi = QK_PIECES[qt]
                        project_qk(2 * (h + 1) + k, lo, hi)
                    if g >= G:
                        project_out(g - G)
                    if g >= 6 and g % 4 == 2:
                        probs_v((g - 6) // 4)
                    if g == 55:
                        pe.wait_ge(s_qklow, 16 * n + 16)
                        group_mean(n + 1, 0)
                    if g == 56:
                        group_spread(n + 1, 0)
                    if g == 62:
                        group_mean(n + 1, 1)
                    if g == 63:
                        group_spread(n + 1, 1)
                for j in range(3, NP):
                    project_out(j)


def kernel(x, L0_conv_norm_w, L0_conv_norm_b, L0_conv_qkv_w, L0_conv_qkv_b, L0_conv_proj_w, L0_conv_proj_b,
           L1_conv_gn_scale, L1_conv_gn_bias, L1_conv_wq, L1_conv_bq, L1_conv_wk, L1_conv_bk, L1_conv_wv, L1_conv_bv,
           L1_conv_wp, L1_conv_bp):
    import numpy as np
    import concourse.bacc as bacc
    from concourse.bass_utils import run_bass_kernel_spmd

    w0 = np.asarray(L0_conv_qkv_w).reshape(HEADS, 3, CH, C)
    b0 = np.asarray(L0_conv_qkv_b).reshape(HEADS, 3, CH)
    layers = [
        (w0[:, 0], w0[:, 1], w0[:, 2], L0_conv_proj_w, b0[:, 0], b0[:, 1], b0[:, 2], L0_conv_proj_b,
         L0_conv_norm_w, L0_conv_norm_b),
        tuple(np.asarray(a).reshape(HEADS, CH, C) for a in (L1_conv_wq, L1_conv_wk, L1_conv_wv)) + (L1_conv_wp,)
        + tuple(np.asarray(a).reshape(HEADS, CH) for a in (L1_conv_bq, L1_conv_bk, L1_conv_bv)) + (L1_conv_bp,
         L1_conv_gn_scale, L1_conv_gn_bias),
    ]
    weights, params, gn_params = [], [], []
    for wq, wk, wv, wp, bq, bk, bv, bp, gw, gb in layers:
        qk = np.concatenate([wq, wk], axis=1).reshape(HEADS, P, CT, P).transpose(0, 3, 2, 1).reshape(HEADS, P, HALF)
        v = np.asarray(wv).reshape(C, CT, P).transpose(1, 2, 0)
        p = np.asarray(wp).reshape(CT, P, CT, P).transpose(0, 3, 2, 1).reshape(CT, P, HALF)
        units = np.concatenate([qk, v, p], axis=0)
        weights.append(units.reshape(CHUNKS, 2, P, HALF).transpose(0, 2, 1, 3).reshape(CHUNKS, P, 2 * HALF))
        par = np.zeros((P, 20), np.float32)
        par[:, 0:HEADS] = np.concatenate([bq, bk], axis=1).T
        par[0:CH, HEADS:2 * HEADS] = np.asarray(bv).T
        par[:, 2 * HEADS:] = np.asarray(bp).reshape(CT, P).T
        params.append(par)
        gn_params.append(np.concatenate([np.asarray(gw).reshape(CT, P).T, np.asarray(gb).reshape(CT, P).T], axis=1))
    consts = np.stack([np.eye(P), np.kron(np.eye(P // GROUP), np.full((GROUP, GROUP), 1.0 / GROUP))], axis=1)

    arrays = {
        "x": np.ascontiguousarray(np.asarray(x).reshape(B, C, T)),
        "weights": np.ascontiguousarray(np.stack(weights)),
        "params": np.ascontiguousarray(np.stack(params)),
        "gn_params": np.ascontiguousarray(np.stack(gn_params)),
        "consts": np.ascontiguousarray(consts.astype(np.float32)),
    }
    nc = bacc.Bacc("TRN2", target_bir_lowering=False, num_devices=1)
    ins = [nc.dram_tensor(name, a.shape, F32, kind="ExternalInput").ap() for name, a in arrays.items()]
    hidden = nc.dram_tensor("hidden", (B, C, T), F32, kind="Internal").ap()
    split = nc.dram_tensor("split", (LAYERS, UNITS, P, 2 * HALF), F32, kind="Internal").ap()
    out = nc.dram_tensor("out", (B, C, T), F32, kind="ExternalOutput").ap()
    attention_blocks(nc, *ins, hidden, split, out)
    r = run_bass_kernel_spmd(nc, [arrays], core_ids=[0])
    return r.results[0]["out"].reshape(B, C, 32, 32)
```

```python
from contextlib import ExitStack

import concourse.bass as bass
from concourse import mybir

F32 = mybir.dt.float32
F32R = mybir.dt.float32r
ALU = mybir.AluOpType
ACT = mybir.ActivationFunctionType
AX = mybir.AxisListType

P = 128
LAYERS, B, C, T = 2, 8, 512, 1024
N = LAYERS * B
HEADS, CH = 8, 64
GROUP = 16
CT = C // P
QT = T // P
G = HEADS * QT
LAG = 3
HALF = 512
NG = G // 4
NP = 2 * CT
SCALE = CH ** -0.5
EPS = 1e-5
UNITS = HEADS + 2 * CT
RAW = 4
AHEAD = CT + 1
PIECE = 3
RES = 3
RES_PER = [len(range(s, NP, RES)) for s in range(RES)]
USES = [("qk", h) for h in range(1, HEADS)] + [("out", o) for o in range(CT)] + [("qk", 0)] + [("v", c) for c in range(CT)]
FIRST_NEXT = USES.index(("qk", 0))
FIRST_V = USES.index(("v", 0))
SPLIT_AT = {8 * (i - 1) + 4: i for i in range(1, HEADS - 1)} | {45: 7, 48: 8, 49: 9, 52: 10, 53: 11}
APPLY_AT = {56: 0, 57: 1, 61: 2, 64: 3}
HIGH_AT = {57: 0, 58: 1, 62: 2, 65: 3}
LOW_AT = {58: 0, 60: 1, 62: 2, 65: 3}
TERMS = ((0, 0), (0, 1), (1, 0))


def attention_blocks(nc, x, weights, qk_params, params, gn_params, consts, hidden, out):
    ctx = ExitStack()
    with ctx:
        def sb(name, shape, dt=F32):
            return ctx.enter_context(nc.sbuf_tensor(name, shape, dt))

        def sem(name):
            return ctx.enter_context(nc.semaphore(name))

        raw = sb("raw", [P, RAW, HALF])
        wqk = sb("wqk", [P, 2, 2, HALF], F32R)
        wvp = sb("wvp", [P, CT, 2, HALF], F32R)
        xin = sb("xin", [P, CT, T])
        xn = sb("xn", [P, 2, CT, T], F32R)
        va = sb("va", [P, CT + 1, 2 * T], F32R)
        q_hl = sb("q_hl", [P, 2, T], F32R)
        q_lh = sb("q_lh", [P, 2, T], F32R)
        k_lh = sb("k_lh", [P, 2, T], F32R)
        probs = sb("probs", [P, LAG, T])
        probs_t = sb("probs_t", [P, 2, QT, HALF], F32R)
        head_out = sb("head_out", [P, HALF])
        res = sb("res", [P, RES, HALF])
        cst = sb("cst", [P, 2, P])
        par = sb("par", [P, HEADS + CT])
        qk_bias = sb("qk_bias", [P, HEADS])
        neg_top = sb("neg_top", [P, 4])
        gn_par = sb("gn_par", [P, 2 * CT])
        neg_max = sb("neg_max", [P, 4])
        row_sum = sb("row_sum", [P, 4])
        row_inv = sb("row_inv", [P, 4])
        bn_part = sb("bn_part", [P, CT, 2, 6])
        bn_mv = sb("bn_mv", [P, CT, 2])
        g_mean = sb("g_mean", [P, CT])
        g_dev = sb("g_dev", [P, CT])
        g_sq = sb("g_sq", [P, CT])
        g_spread = sb("g_spread", [P, CT])
        g_var = sb("g_var", [P, CT])
        minus_half = sb("minus_half", [P, CT])
        g_rstd = sb("g_rstd", [P, CT])
        g_scale = sb("g_scale", [P, CT])
        g_ms = sb("g_ms", [P, CT])
        g_shift = sb("g_shift", [P, CT])
        ident = cst[:, 0, :]
        gmat = cst[:, 1, :]

        ps_s = ctx.enter_context(nc.psum_tensor("ps_s", [P, 4, HALF], F32))
        ps_t = ctx.enter_context(nc.psum_tensor("ps_t", [P, 2, HALF], F32))
        ps_pv = ctx.enter_context(nc.psum_tensor("ps_pv", [P, HALF], F32))
        ps_qk = ctx.enter_context(nc.psum_tensor("ps_qk", [P, HALF], F32))

        v_view = va[:, 1:CT + 1, :].rearrange("p r (h t c) -> p (r h) t c", h=2, t=QT)
        a_view = va[:, 0:CT, :].rearrange("p r (w t) -> p r w t", w=2)

        s_const = sem("s_const")
        s_par = sem("s_par")
        s_gnpar = sem("s_gnpar")
        s_half = sem("s_half")
        s_qkbias = sem("s_qkbias")
        s_raw = [sem(f"s_raw{i}") for i in range(RAW)]
        s_whigh = sem("s_whigh")
        s_wlow = sem("s_wlow")
        s_x = [sem(f"s_x{i}") for i in range(CT)]
        s_stats = sem("s_stats")
        s_gmean = sem("s_gmean")
        s_spread = sem("s_spread")
        s_gspread = sem("s_gspread")
        s_gvar = sem("s_gvar")
        s_shift = sem("s_shift")
        s_applied = sem("s_applied")
        s_xhigh = sem("s_xhigh")
        s_xlow = sem("s_xlow")
        s_dve = sem("s_dve")
        s_pool = sem("s_pool")
        s_qk = sem("s_qk")
        s_qkhigh = sem("s_qkhigh")
        s_qklow = sem("s_qklow")
        s_swap = [[sem(f"s_swap{s}{k}") for k in range(2)] for s in range(2)]
        s_v = sem("s_v")
        s_vhigh = sem("s_vhigh")
        s_vlow = sem("s_vlow")
        s_score = sem("s_score")
        s_top = sem("s_top")
        s_max = sem("s_max")
        s_exp = sem("s_exp")
        s_inv = sem("s_inv")
        s_norm = sem("s_norm")
        s_trans = sem("s_trans")
        s_phigh = sem("s_phigh")
        s_plow = sem("s_plow")
        s_pv = sem("s_pv")
        s_olow = sem("s_olow")
        s_osum = sem("s_osum")
        s_ohigh = sem("s_ohigh")
        s_o = sem("s_o")
        s_proj = sem("s_proj")
        s_y = sem("s_y")
        s_res = [sem(f"s_res{i}") for i in range(RES)]
        s_out = [sem(f"s_out{i}") for i in range(RES)]

        def image(t, b):
            return t[b].rearrange("(ct p) n -> p ct n", p=P)

        raw_ahead = [len([i for i in range(FIRST_NEXT, UNITS) if i % RAW == s]) for s in range(RAW)]

        def unit_parts(i):
            kind, at = USES[i]
            return wqk[:, at % 2] if kind == "qk" else wvp[:, at]

        def units_done(n, i):
            return UNITS * n + AHEAD + i + 1

        def qk_piece(g):
            i, lo = 2 + (g + 1) // 4, PIECE * ((g + 1) % 4)
            return (i, lo, lo + PIECE) if i < 2 * HEADS else None

        def exp_early(g):
            return 6 <= g < G and g % 4 == 2

        def wait_apart(eng, *waits):
            for _, value in waits:
                if not isinstance(value, int):
                    eng.compute_val(value)
            eng.wait_ge(s_const, 16)
            for semaphore, value in waits:
                eng.wait_ge(semaphore, value)

        block = ctx.enter_context(nc.Block())

        @block.sync
        def _(sp):
            def swap_q(n, h, k):
                sp.wait_ge(s_qklow, 2 * HEADS * n + 2 * h + k + 1)
                s, cols = h % 2, slice(HALF * k, HALF * k + HALF)
                for to, of in ((slice(0, CH), slice(CH, P)), (slice(CH, P), slice(0, CH))):
                    sp.dma_start(q_lh[to, s, cols].bitcast(F32), q_hl[of, s, cols].bitcast(F32)).then_inc(s_swap[s][k], 16)

            def load_unit(n, i, layer):
                kind, at = USES[i]
                unit = {"qk": at, "v": HEADS + at, "out": HEADS + CT + at}[kind]
                sp.dma_start(raw[:, i % RAW, :], weights[layer, unit]).then_inc(s_raw[i % RAW], 16)

            def next_unit(n, i):
                wait_apart(sp, (s_wlow, units_done(n, i - RAW)))
                load_unit(n, i, n // B if i < FIRST_NEXT else (n + 1) // B % LAYERS)

            for ct in range(CT):
                sp.dma_start(xin[:, ct, :], image(x, 0)[:, ct, :]).then_inc(s_x[ct], 16)
                if ct == 0:
                    sp.dma_start(cst[:, :, :], consts).then_inc(s_const, 16)
                    sp.dma_start(gn_par[:, :], gn_params[0]).then_inc(s_gnpar, 16)
            sp.dma_start(qk_bias[:, :], qk_params[0]).then_inc(s_qkbias, 16)
            for i in range(FIRST_NEXT, UNITS - 1):
                load_unit(-1, i, 0)
            sp.dma_start(par[:, :], params[0]).then_inc(s_par, 16)
            sp.wait_ge(s_wlow, 1)
            load_unit(-1, UNITS - 1, 0)

            with sp.Fori(0, N) as n:
                nxt = (n + 1) // B % LAYERS
                swap_q(n, 0, 0)
                swap_q(n, 0, 1)
                wait_apart(sp, (s_xlow, 2 * CT * (n + 1)))
                sp.dma_start(gn_par[:, :], gn_params[nxt]).then_inc(s_gnpar, 16)
                with sp.If(n + 1 < B):
                    for ct in range(CT):
                        sp.dma_start(xin[:, ct, :], image(x, (n + 1) % B)[:, ct, :]).then_inc(s_x[ct], 16)
                with sp.Else():
                    for ct in range(CT):
                        sp.dma_start(xin[:, ct, :], image(hidden, (n + 1) % B)[:, ct, :]).then_inc(s_x[ct], 16)

                def load_res(j):
                    o, k, s = j % CT, j // CT, j % RES
                    src = slice(k * HALF, (k + 1) * HALF)
                    if j >= RES:
                        wait_apart(sp, (s_out[s], 16 * (RES_PER[s] * n + j // RES)))
                    with sp.If(n < B):
                        sp.dma_start(res[:, s, :], image(x, n % B)[:, o, src]).then_inc(s_res[s], 16)
                    with sp.Else():
                        sp.dma_start(res[:, s, :], image(hidden, n % B)[:, o, src]).then_inc(s_res[s], 16)

                def store_res(j):
                    o, k, s = j % CT, j // CT, j % RES
                    dst = slice(k * HALF, (k + 1) * HALF)
                    wait_apart(sp, (s_y, NP * n + j + 1))
                    with sp.If(n < B):
                        sp.dma_start(image(hidden, n % B)[:, o, dst], res[:, s, :]).then_inc(s_out[s], 16)
                    with sp.Else():
                        sp.dma_start(image(out, n % B)[:, o, dst], res[:, s, :]).then_inc(s_out[s], 16)

                for i in range(5):
                    next_unit(n, i)
                for j in range(RES):
                    load_res(j)
                for h in range(1, 6):
                    swap_q(n, h, 0)
                    next_unit(n, h + 4)
                    swap_q(n, h, 1)
                swap_q(n, 6, 0)
                next_unit(n, 10)
                next_unit(n, 11)
                swap_q(n, 6, 1)
                next_unit(n, 12)
                next_unit(n, 13)
                swap_q(n, 7, 0)
                next_unit(n, 14)
                next_unit(n, 15)
                swap_q(n, 7, 1)
                sp.dma_start(qk_bias[:, :], qk_params[nxt]).then_inc(s_qkbias, 16)
                for j in range(NP):
                    store_res(j)
                    if 1 <= j and j + 2 < NP:
                        load_res(j + 2)
                sp.dma_start(par[:, :], params[nxt]).then_inc(s_par, 16)
                wait_apart(sp, *((s_out[s], 16 * RES_PER[s] * (n + 1)) for s in range(RES)))
            sp.wait_ge(s_par, 16 * (N + 1))
            sp.wait_ge(s_qkbias, 16 * (N + 1))
            for ct in range(CT):
                sp.wait_ge(s_x[ct], 16 * (N + 1))

        @block.gpsimd
        def _(pool):
            PER_GN = 3

            def gn_coeffs(m):
                c = PER_GN * m
                pool.wait_ge(s_gnpar, 16 * m + 16)
                pool.wait_ge(s_gvar, m + 1)
                nc.gpsimd.tensor_tensor(g_rstd[:, :], g_var[:, :], minus_half[:, :], ALU.pow).then_inc(s_pool, 1)
                pool.wait_ge(s_pool, c + 1)
                nc.gpsimd.tensor_tensor(g_scale[:, :], g_rstd[:, :], gn_par[:, 0:CT], ALU.mult).then_inc(s_pool, 1)
                pool.wait_ge(s_pool, c + 2)
                nc.gpsimd.tensor_tensor(g_ms[:, :], g_mean[:, :], g_scale[:, :], ALU.mult).then_inc(s_pool, 1)
                pool.wait_ge(s_pool, c + 3)
                nc.gpsimd.tensor_tensor(g_shift[:, :], gn_par[:, CT:2 * CT], g_ms[:, :], ALU.subtract).then_inc(s_shift, 1)

            def gn_apply(m, ct):
                wait_apart(pool, (s_shift, m + 1))
                nc.gpsimd.tensor_scalar(xin[:, ct, :], xin[:, ct, :], g_scale[:, ct:ct + 1], g_shift[:, ct:ct + 1],
                                        ALU.mult, ALU.add).then_inc(s_applied, 1)

            def gn_low(m, i):
                ct, cols = i // 2, slice(HALF * (i % 2), HALF * (i % 2) + HALF)
                pool.wait_ge(s_xhigh, CT * m + ct + 1)
                nc.gpsimd.tensor_tensor(xn[:, 1, ct, cols], xin[:, ct, cols], xn[:, 0, ct, cols].bitcast(F32),
                                        ALU.subtract).then_inc(s_xlow, 1)

            def weight_low(n, i):
                pool.wait_ge(s_whigh, units_done(n, i))
                parts = unit_parts(i)
                nc.gpsimd.tensor_tensor(parts[:, 1, :], raw[:, i % RAW, :], parts[:, 0, :].bitcast(F32),
                                        ALU.subtract).then_inc(s_wlow, 1)

            pool.wait_ge(s_half, 1)
            gn_coeffs(0)
            for ct in range(CT):
                gn_apply(0, ct)
                gn_low(0, 2 * ct)
                gn_low(0, 2 * ct + 1)
            for i in range(FIRST_NEXT, UNITS):
                weight_low(-1, i)

            with pool.Fori(0, N) as n:
                def normalise(g):
                    s = g % LAG
                    wait_apart(pool, (s_inv, G * n + g + 1))
                    nc.gpsimd.tensor_scalar(probs[:, s, :], probs[:, s, :], row_inv[:, g % 4:g % 4 + 1], 1.0,
                                            ALU.mult, ALU.mult).then_inc(s_norm, 1)

                def split_out(k, before, count):
                    h = k // 2
                    r = slice(CH * (h % 2), CH * (h % 2) + CH)
                    cols = slice(HALF * (k % 2), HALF * (k % 2) + HALF)
                    wait_apart(pool, (before, count), (s_osum, NG * n + k + 1))
                    nc.gpsimd.tensor_scalar(a_view[r, h // 2, 0, cols], head_out[r, :], 1.0, 1.0,
                                            ALU.mult, ALU.mult).then_inc(s_ohigh, 1)
                    pool.wait_ge(s_ohigh, NG * n + k + 1)
                    nc.gpsimd.tensor_tensor(a_view[r, h // 2, 1, cols], head_out[r, :],
                                            a_view[r, h // 2, 0, cols].bitcast(F32), ALU.subtract).then_inc(s_o, 1)
                    wait_apart(pool, (s_o, NG * n + k + 1))

                weight_low(n, 0)
                for g in range(G + LAG):
                    if 1 <= g <= G:
                        normalise(g - 1)
                    if g >= 7 and g % 4 == 3:
                        split_out((g - 7) // 4, s_norm, G * n + g)
                    if g in SPLIT_AT:
                        weight_low(n, SPLIT_AT[g])
                    if g == 54:
                        gn_coeffs(n + 1)
                    if g in APPLY_AT:
                        gn_apply(n + 1, APPLY_AT[g])
                    if g in LOW_AT:
                        gn_low(n + 1, LOW_AT[g])
                split_out(NG - 1, s_xlow, 2 * CT * (n + 1) + len(LOW_AT))
                for i in range(len(LOW_AT), 2 * CT):
                    gn_low(n + 1, i)
                for i in range(FIRST_V, UNITS):
                    weight_low(n, i)

        @block.scalar
        def _(act):
            def gn_high(m, ct):
                act.wait_ge(s_applied, CT * m + ct + 1)
                nc.scalar.activation(xn[:, 0, ct, :], xin[:, ct, :], ACT.Copy).then_inc(s_xhigh, 1)

            def weight_high(n, i):
                s = i % RAW
                act.wait_ge(s_raw[s], 16 * (UNITS // RAW * n + raw_ahead[s] + i // RAW + 1))
                nc.scalar.activation(unit_parts(i)[:, 0, :], raw[:, s, :], ACT.Copy).then_inc(s_whigh, 1)

            for i in range(FIRST_NEXT, UNITS - 1):
                weight_high(-1, i)
            for ct in range(CT):
                gn_high(0, ct)
            weight_high(-1, UNITS - 1)

            with act.Fori(0, N) as n:
                def qk_high(i):
                    h, k = i // 2, i % 2
                    cols = slice(HALF * k, HALF * k + HALF)
                    act.wait_ge(s_qk, 16 * n + i + 1)
                    if i == 0:
                        act.wait_ge(s_qkbias, 16 * n + 16)
                    nc.scalar.activation(q_hl[0:CH, h % 2, cols], ps_qk[0:CH, :], ACT.Identity,
                                         bias=qk_bias[0:CH, h:h + 1])
                    nc.scalar.activation(k_lh[CH:P, h % 2, cols], ps_qk[CH:P, :], ACT.Identity,
                                         bias=qk_bias[CH:P, h:h + 1]).then_inc(s_qkhigh, 1)

                def v_high(t):
                    act.wait_ge(s_v, QT * n + t + 1)
                    nc.scalar.activation(v_view[:, :, t, 0:CH], ps_s[:, t % 4, :].rearrange("p (h c) -> p h c", h=HEADS),
                                         ACT.Copy).then_inc(s_vhigh, 1)

                def exp(g):
                    b = 2 * (g % 2)
                    act.wait_ge(s_max, G * n + g + 1)
                    nc.scalar.activation(probs[:, g % LAG, :].rearrange("p (b n) -> p b n", b=2), ps_s[:, b:b + 2, :],
                                         ACT.Exp, bias=neg_max[:, g % 4:g % 4 + 1], scale=SCALE,
                                         accum_out=row_sum[:, g % 4:g % 4 + 1]).then_inc(s_exp, 1)

                def probs_high(g, b):
                    act.wait_ge(s_trans, 2 * G * n + 2 * g + b + 1)
                    if g % 4 == 0 and b == 0 and g:
                        act.wait_ge(s_pv, NG * n + g // 4)
                    q = P * (g % 4)
                    nc.scalar.activation(probs_t[:, 0, 4 * b:4 * b + 4, q:q + P],
                                         ps_t[:, b, :].rearrange("p (k q) -> p k q", k=4), ACT.Copy).then_inc(s_phigh, 1)

                def out_low_half(k):
                    act.wait_ge(s_pv, NG * n + k + 1)
                    if k:
                        act.wait_ge(s_o, NG * n + k)
                    nc.scalar.activation(head_out[0:CH, :], ps_pv[CH:P, :], ACT.Copy).then_inc(s_olow, 1)

                qk_high(0)
                v_high(0)
                v_high(1)
                qk_high(1)
                for t in range(2, QT - 1):
                    v_high(t)
                    if t == 2:
                        weight_high(n, 0)
                for g in range(G + LAG):
                    qt, h = g % QT, g // QT
                    if g >= LAG:
                        probs_high(g - LAG, 0)
                        probs_high(g - LAG, 1)
                    if g >= 7 and g % 4 == 3:
                        out_low_half((g - 7) // 4)
                    if 1 <= g <= G and not exp_early(g - 1):
                        exp(g - 1)
                    if g == 1:
                        v_high(QT - 1)
                    if qk_piece(g) and qk_piece(g)[2] == 3 * CT:
                        qk_high(qk_piece(g)[0])
                    if exp_early(g):
                        exp(g)
                    if g in SPLIT_AT:
                        weight_high(n, SPLIT_AT[g])
                    if g in HIGH_AT:
                        gn_high(n + 1, HIGH_AT[g])
                out_low_half(NG - 1)
                for ct in range(CT):
                    act.wait_ge(s_proj, NP * n + CT + ct + 1)
                    weight_high(n, FIRST_V + ct)

        @block.vector
        def _(dve):
            PER_GN = 4

            def gn_stats(m, ct):
                dve.wait_ge(s_x[ct], 16 * m + 16)
                for k in range(2):
                    last = nc.vector.bn_stats(bn_part[:, ct, k, :], xin[:, ct, HALF * k:HALF * k + HALF])
                if ct == CT - 1:
                    last.then_inc(s_dve, 1)
                    wait_apart(dve, (s_dve, PER_GN * m + 1))
                    for i in range(CT):
                        last = nc.vector.bn_aggr(bn_mv[:, i, :], bn_part[:, i, :, :].rearrange("p k s -> p (k s)"))
                    last.then_inc(s_stats, 1)

            def gn_spread(m):
                c = PER_GN * m
                dve.wait_ge(s_gmean, m + 1)
                nc.vector.tensor_copy(g_mean[:, :], ps_pv[:, 0:CT]).then_inc(s_dve, 1)
                dve.wait_ge(s_dve, c + 2)
                nc.vector.tensor_tensor(g_dev[:, :], bn_mv[:, :, 0], g_mean[:, :], ALU.subtract).then_inc(s_dve, 1)
                dve.wait_ge(s_dve, c + 3)
                nc.vector.tensor_tensor(g_sq[:, :], g_dev[:, :], g_dev[:, :], ALU.mult).then_inc(s_dve, 1)
                dve.wait_ge(s_dve, c + 4)
                nc.vector.tensor_tensor(g_spread[:, :], g_sq[:, :], bn_mv[:, :, 1], ALU.add).then_inc(s_spread, 1)

            def gn_var(m):
                dve.wait_ge(s_gspread, m + 1)
                nc.vector.tensor_scalar(g_var[:, :], ps_pv[:, CT:2 * CT], EPS, None, ALU.add).then_inc(s_gvar, 1)

            nc.vector.memset(minus_half[:, :], -0.5).then_inc(s_half, 1)
            for ct in range(CT):
                gn_stats(0, ct)
            gn_spread(0)
            gn_var(0)

            with dve.Fori(0, N) as n:
                def qk_low(i):
                    h, k = i // 2, i % 2
                    cols = slice(HALF * k, HALF * k + HALF)
                    dve.wait_ge(s_qkhigh, 16 * n + i + 1)
                    nc.vector.scalar_tensor_tensor(q_hl[CH:P, h % 2, cols], ps_qk[0:CH, :], qk_bias[0:CH, h:h + 1],
                                                   q_hl[0:CH, h % 2, cols].bitcast(F32), ALU.add, ALU.subtract)
                    nc.vector.scalar_tensor_tensor(k_lh[0:CH, h % 2, cols], ps_qk[CH:P, :], qk_bias[CH:P, h:h + 1],
                                                   k_lh[CH:P, h % 2, cols].bitcast(F32),
                                                   ALU.add, ALU.subtract).then_inc(s_qklow, 1)

                def v_low(t):
                    dve.wait_ge(s_vhigh, QT * n + t + 1)
                    nc.vector.tensor_tensor(v_view[:, :, t, CH:P], ps_s[:, t % 4, :].rearrange("p (h c) -> p h c", h=HEADS),
                                            v_view[:, :, t, 0:CH].bitcast(F32), ALU.subtract).then_inc(s_vlow, 1)

                def row_top(g):
                    b = 2 * (g % 2)
                    dve.wait_ge(s_score, G * n + g + 1)
                    nc.vector.reduce_max(neg_top[:, g % 4:g % 4 + 1], ps_s[:, b:b + 2, :], AX.XY,
                                         negate=True).then_inc(s_top, 1)

                def row_max(g):
                    dve.wait_ge(s_top, G * n + g + 1)
                    nc.vector.tensor_scalar(neg_max[:, g % 4:g % 4 + 1], neg_top[:, g % 4:g % 4 + 1], SCALE, None,
                                            ALU.mult).then_inc(s_max, 1)

                def row_inverse(g):
                    dve.wait_ge(s_exp, G * n + g + 1)
                    nc.vector.reciprocal(row_inv[:, g % 4:g % 4 + 1], row_sum[:, g % 4:g % 4 + 1]).then_inc(s_inv, 1)

                def probs_low(g, b):
                    dve.wait_ge(s_phigh, 2 * G * n + 2 * g + b + 1)
                    q = P * (g % 4)
                    nc.vector.tensor_tensor(probs_t[:, 1, 4 * b:4 * b + 4, q:q + P],
                                            ps_t[:, b, :].rearrange("p (k q) -> p k q", k=4),
                                            probs_t[:, 0, 4 * b:4 * b + 4, q:q + P].bitcast(F32),
                                            ALU.subtract).then_inc(s_plow, 1)

                def out_sum(k):
                    h = k // 2
                    r = slice(CH * (h % 2), CH * (h % 2) + CH)
                    dve.wait_ge(s_olow, NG * n + k + 1)
                    nc.vector.scalar_tensor_tensor(head_out[r, :], ps_pv[0:CH, :], par[0:CH, h:h + 1],
                                                   head_out[0:CH, :], ALU.add, ALU.add).then_inc(s_osum, 1)

                def add_residual(j):
                    o, s = j % CT, j % RES
                    dve.wait_ge(s_proj, NP * n + j + 1)
                    dve.wait_ge(s_res[s], 16 * (RES_PER[s] * n + j // RES + 1))
                    nc.vector.scalar_tensor_tensor(res[:, s, :], ps_s[:, j % 4, :], par[:, HEADS + o:HEADS + o + 1],
                                                   res[:, s, :], ALU.add, ALU.add).then_inc(s_y, 1)

                qk_low(0)
                v_low(0)
                v_low(1)
                qk_low(1)
                for t in range(2, QT - 1):
                    v_low(t)
                    if t >= QT - 1 - CT:
                        gn_stats(n + 1, t - (QT - 1 - CT))
                for g in range(G + LAG):
                    if g == 53:
                        gn_spread(n + 1)
                    if g == 54:
                        gn_var(n + 1)
                    if g >= LAG:
                        probs_low(g - LAG, 0)
                        probs_low(g - LAG, 1)
                    if g >= 7 and g % 4 == 3:
                        out_sum((g - 7) // 4)
                    if 1 <= g <= G and not exp_early(g - 1):
                        row_inverse(g - 1)
                    if g < G:
                        row_top(g)
                        row_max(g)
                    if g == 0:
                        v_low(QT - 1)
                    if qk_piece(g) and qk_piece(g)[2] == 3 * CT:
                        qk_low(qk_piece(g)[0])
                    if exp_early(g):
                        row_inverse(g)
                    if g > G:
                        add_residual(g - G - 1)
                add_residual(2)
                out_sum(NG - 1)
                for j in range(3, NP):
                    add_residual(j)

        @block.tensor
        def _(pe):
            def group_mean(m):
                pe.wait_ge(s_stats, m + 1)
                nc.tensor.matmul(ps_pv[:, 0:CT], gmat, bn_mv[:, :, 0], start=True, stop=True).then_inc(s_gmean, 1)

            def group_spread(m):
                pe.wait_ge(s_spread, m + 1)
                nc.tensor.matmul(ps_pv[:, CT:2 * CT], gmat, g_spread[:, :], start=True, stop=True).then_inc(s_gspread, 1)

            pe.wait_ge(s_const, 16)
            group_mean(0)
            group_spread(0)

            with pe.Fori(0, N) as n:
                def project_qk(i, lo, hi):
                    h, k = i // 2, i % 2
                    if k == 0 and lo == 0:
                        pe.wait_ge(s_wlow, units_done(n, h - 1 if h else FIRST_NEXT - UNITS))
                    if lo == 0 and i > 0:
                        pe.wait_ge(s_qklow, 16 * n + i)
                    for j in range(lo, hi):
                        w, v = TERMS[j // CT]
                        last = nc.tensor.matmul(ps_qk[:, :], wqk[:, h % 2, w, P * (j % CT):P * (j % CT) + P], xn[:, v, j % CT, HALF * k:HALF * k + HALF],
                                                start=j == 0, stop=j == 3 * CT - 1)
                    if hi == 3 * CT:
                        last.then_inc(s_qk, 1)

                def project_v(t):
                    if t == 3:
                        pe.wait_ge(s_par, 16 * n + 16)
                    if t >= 4:
                        pe.wait_ge(s_vlow, QT * n + t - 3)
                    if t == 0:
                        pe.wait_ge(s_wlow, units_done(n, -1))
                    for j in range(3 * CT):
                        w, v = TERMS[j // CT]
                        last = nc.tensor.matmul(ps_s[:, t % 4, :], xn[:, v, j % CT, P * t:P * t + P], wvp[:, j % CT, w, :],
                                                start=j == 0, stop=j == 3 * CT - 1)
                    last.then_inc(s_v, 1)

                def scores(g):
                    h, qt, b = g // QT, g % QT, 2 * (g % 2)
                    s = h % 2
                    if qt == 0:
                        pe.wait_ge(s_qklow, 2 * HEADS * n + 2 * h + 2)
                    if qt in (0, 4):
                        pe.wait_ge(s_swap[s][qt // 4], 32 * (HEADS // 2 * n + h // 2 + 1))
                    if g < 2:
                        pe.wait_ge(s_vlow, QT * n + 6 + 2 * g)
                    else:
                        pe.wait_ge(s_exp, G * n + g - 1)
                    for q, first in ((q_hl, True), (q_lh, False)):
                        for k in range(2):
                            last = nc.tensor.matmul(ps_s[:, b + k, :], q[:, s, P * qt:P * qt + P],
                                                    k_lh[:, s, HALF * k:HALF * k + HALF], start=first, stop=not first)
                    last.then_inc(s_score, 1)

                def transpose(g):
                    pe.wait_ge(s_norm, G * n + g + 1)
                    for b in range(2):
                        if g:
                            pe.wait_ge(s_plow, 2 * G * n + 2 * g + b - 1)
                        for k in range(4):
                            c = 4 * b + k
                            last = nc.tensor.transpose(ps_t[:, b, P * k:P * k + P], probs[:, g % LAG, P * c:P * c + P], ident)
                        last.then_inc(s_trans, 1)

                def probs_v(k):
                    h = k // 2
                    if k == 0:
                        pe.wait_ge(s_vlow, QT * n + QT)
                    if k:
                        pe.wait_ge(s_osum, NG * n + k)
                    if k == 12:
                        pe.wait_ge(s_gvar, n + 2)
                    for kt in range(QT):
                        if kt in (0, 4):
                            pe.wait_ge(s_plow, 2 * G * n + 8 * k + 7 + kt // 4)
                        for w in range(2):
                            last = nc.tensor.matmul(ps_pv[:, :], v_view[:, h, kt, :], probs_t[:, w, kt, :],
                                                    start=kt == 0 and w == 0, stop=kt == QT - 1 and w == 1)
                    last.then_inc(s_pv, 1)

                def project_out(j, lo=0, hi=3 * CT):
                    o, k = j % CT, j // CT
                    if lo == 0:
                        if j in (0, 2):
                            pe.wait_ge(s_exp, G * n + G - 1 + j // 2)
                        if j < 4:
                            pe.wait_ge(s_wlow, units_done(n, HEADS - 1 + o))
                        else:
                            pe.wait_ge(s_y, NP * n + j - 3)
                    for i in range(lo, hi):
                        ct, (w, v) = i // 3, TERMS[i % 3]
                        if i == 3 * (CT - 1):
                            pe.wait_ge(s_o, NG * n + NG - 1 + k)
                        last = nc.tensor.matmul(ps_s[:, j % 4, :], wvp[:, o, w, P * ct:P * ct + P],
                                                a_view[:, ct, v, HALF * k:HALF * k + HALF], start=i == 0, stop=i == 3 * CT - 1)
                    if hi == 3 * CT:
                        last.then_inc(s_proj, 1)

                pe.wait_ge(s_xlow, 2 * CT * (n + 1))
                project_qk(0, 0, 3 * CT)
                project_v(0)
                project_v(1)
                project_qk(1, 0, 3 * CT)
                for t in range(2, QT - 1):
                    project_v(t)
                project_qk(*qk_piece(-1))
                early, last = 3 * (CT - 1), 3 * CT
                for g in range(G + LAG):
                    if g >= LAG:
                        transpose(g - LAG)
                    if g < G:
                        scores(g)
                    if g == 0:
                        project_v(QT - 1)
                    if qk_piece(g):
                        project_qk(*qk_piece(g))
                    if g == G:
                        project_out(0, 0, early)
                    if g == G + 1:
                        project_out(1, 0, early)
                        project_out(0, early, last)
                    if g == G + 2:
                        project_out(1, early, last)
                        project_out(2)
                    if g >= 6 and g % 4 == 2:
                        probs_v((g - 6) // 4)
                    if g == 52:
                        pe.wait_ge(s_osum, NG * n + 12)
                        group_mean(n + 1)
                    if g == 53:
                        group_spread(n + 1)
                for j in range(3, NP):
                    project_out(j)
                pe.wait_ge(s_y, NP * n + NP - 1)


def kernel(x, L0_conv_norm_w, L0_conv_norm_b, L0_conv_qkv_w, L0_conv_qkv_b, L0_conv_proj_w, L0_conv_proj_b,
           L1_conv_gn_scale, L1_conv_gn_bias, L1_conv_wq, L1_conv_bq, L1_conv_wk, L1_conv_bk, L1_conv_wv, L1_conv_bv,
           L1_conv_wp, L1_conv_bp):
    import numpy as np
    import concourse.bacc as bacc
    from concourse.bass_utils import run_bass_kernel_spmd

    w0 = np.asarray(L0_conv_qkv_w).reshape(HEADS, 3, CH, C)
    b0 = np.asarray(L0_conv_qkv_b).reshape(HEADS, 3, CH)
    layers = [
        (w0[:, 0], w0[:, 1], w0[:, 2], L0_conv_proj_w, b0[:, 0], b0[:, 1], b0[:, 2], L0_conv_proj_b,
         L0_conv_norm_w, L0_conv_norm_b),
        tuple(np.asarray(a).reshape(HEADS, CH, C) for a in (L1_conv_wq, L1_conv_wk, L1_conv_wv)) + (L1_conv_wp,)
        + tuple(np.asarray(a).reshape(HEADS, CH) for a in (L1_conv_bq, L1_conv_bk, L1_conv_bv)) + (L1_conv_bp,
         L1_conv_gn_scale, L1_conv_gn_bias),
    ]
    weights, qk_params, params, gn_params = [], [], [], []
    for wq, wk, wv, wp, bq, bk, bv, bp, gw, gb in layers:
        qk = np.concatenate([wq, wk], axis=1).reshape(HEADS, P, CT, P).transpose(0, 3, 2, 1).reshape(HEADS, P, HALF)
        v = np.asarray(wv).reshape(C, CT, P).transpose(1, 2, 0)
        p = np.asarray(wp).reshape(CT, P, CT, P).transpose(0, 3, 2, 1).reshape(CT, P, HALF)
        weights.append(np.concatenate([qk, v, p], axis=0))
        qk_params.append(np.concatenate([bq, bk], axis=1).T)
        par = np.zeros((P, HEADS + CT), np.float32)
        par[0:CH, 0:HEADS] = np.asarray(bv).T
        par[:, HEADS:] = np.asarray(bp).reshape(CT, P).T
        params.append(par)
        gn_params.append(np.concatenate([np.asarray(gw).reshape(CT, P).T, np.asarray(gb).reshape(CT, P).T], axis=1))
    consts = np.stack([np.eye(P), np.kron(np.eye(P // GROUP), np.full((GROUP, GROUP), 1.0 / GROUP))], axis=1)

    arrays = {
        "x": np.ascontiguousarray(np.asarray(x).reshape(B, C, T)),
        "weights": np.ascontiguousarray(np.stack(weights)),
        "qk_params": np.ascontiguousarray(np.stack(qk_params)),
        "params": np.ascontiguousarray(np.stack(params)),
        "gn_params": np.ascontiguousarray(np.stack(gn_params)),
        "consts": np.ascontiguousarray(consts.astype(np.float32)),
    }
    nc = bacc.Bacc("TRN2", target_bir_lowering=False, num_devices=1)
    ins = [nc.dram_tensor(name, a.shape, F32, kind="ExternalInput").ap() for name, a in arrays.items()]
    hidden = nc.dram_tensor("hidden", (B, C, T), F32, kind="Internal").ap()
    out = nc.dram_tensor("out", (B, C, T), F32, kind="ExternalOutput").ap()
    attention_blocks(nc, *ins, hidden, out)
    r = run_bass_kernel_spmd(nc, [arrays], core_ids=[0])
    return r.results[0]["out"].reshape(B, C, 32, 32)
```

```python
from contextlib import ExitStack

from concourse import mybir

F32 = mybir.dt.float32
F32R = mybir.dt.float32r
ALU = mybir.AluOpType
ACT = mybir.ActivationFunctionType
AX = mybir.AxisListType

P = 128
LAYERS, B, C, T = 2, 8, 512, 1024
N = LAYERS * B
HEADS, CH = 8, 64
GROUP = 16
CT = C // P
QT = T // P
G = HEADS * QT
LAG = 3
HALF = 512
NG = G // 4
NP = 2 * CT
SCALE = CH ** -0.5
EPS = 1e-5
UNITS = HEADS + 2 * CT
RAW = 4
AHEAD = CT + 1
PIECE = 3
K_PUTS, Q_PUTS = 2 * 16, 3 * 16
RES = 3
USES = [("qk", h) for h in range(1, HEADS - CT)]
for step in range(CT):
    USES += [("qk", HEADS - CT + step), ("out", step)]
USES += [("qk", 0)] + [("v", ct) for ct in range(CT)]
FIRST_NEXT = USES.index(("qk", 0))
FIRST_V = USES.index(("v", 0))
SPLIT_AT = {8 * h - 14: USES.index(("qk", h)) for h in range(2, HEADS)}
SPLIT_AT |= {8 * o + 22: USES.index(("out", o)) for o in range(CT)} | {50: FIRST_NEXT}
COPY_AT = {4 * k + 7: k for k in range(NG - 1)}
SUM_AT = {4 * k + (10 if k < NG - 2 else 8): k for k in range(NG - 1)}
PUT_AT = {4 * k + (10 if k < NG - 2 else 8): k for k in range(NG - 1)}
APPLY_AT = {12: 0, 20: 1, 28: 2, 36: 3}
HIGH_AT = {56: (0,), 57: (1,), 60: (2,), 61: (3,), 64: (4, 5), 65: (6, 7)}
LOW_AT = {57: 0, 58: 1, 61: 2, 62: 3}
OUT_PIECE_AT = {55: (0, 0), 56: (0, 1), 57: (0, 2), 59: (1, 0), 60: (1, 1), 61: (1, 2)}
PARTIAL_AT = 58
BIASES_AT = 62
TERMS = ((0, 0), (0, 1), (1, 0))


def attention_blocks(nc, x, weights, qk_params, params, gn_params, consts, hidden, out):
    ctx = ExitStack()
    with ctx:
        def sb(name, shape, dt=F32):
            return ctx.enter_context(nc.sbuf_tensor(name, shape, dt))

        def sem(name):
            return ctx.enter_context(nc.semaphore(name))

        raw = sb("raw", [P, RAW, HALF])
        wqk = sb("wqk", [P, 2, 2, HALF], F32R)
        wvp = sb("wvp", [P, CT, 2, HALF], F32R)
        xin = sb("xin", [P, CT, T])
        xn = sb("xn", [P, 2, CT, T], F32R)
        va = sb("va", [P, CT + 1, 2 * T], F32R)
        qk_full = sb("qk_full", [P, HALF])
        qk_part = sb("qk_part", [P, 2, HALF], F32R)
        q_parts = sb("q_parts", [P, 2, 2, T], F32R)
        k_lh = sb("k_lh", [P, 2, T], F32R)
        probs = sb("probs", [P, LAG, T])
        probs_t = sb("probs_t", [P, 2, QT, HALF], F32R)
        head_out = sb("head_out", [P, 2, HALF])
        res = sb("res", [P, RES, HALF])
        cst = sb("cst", [P, 2, P])
        par = sb("par", [P, HEADS + CT])
        qk_bias = sb("qk_bias", [P, HEADS])
        qk_scale = sb("qk_scale", [P, 1])
        qk_shift = sb("qk_shift", [P, HEADS])
        gn_par = sb("gn_par", [P, 2 * CT])
        neg_max = sb("neg_max", [P, 4])
        row_sum = sb("row_sum", [P, 4])
        row_inv = sb("row_inv", [P, 4])
        bn_part = sb("bn_part", [P, CT, 2, 6])
        bn_mv = sb("bn_mv", [P, CT, 2])
        g_mean = sb("g_mean", [P, CT])
        g_dev = sb("g_dev", [P, CT])
        g_sq = sb("g_sq", [P, CT])
        g_spread = sb("g_spread", [P, CT])
        g_var = sb("g_var", [P, CT])
        minus_half = sb("minus_half", [P, CT])
        g_rstd = sb("g_rstd", [P, CT])
        g_scale = sb("g_scale", [P, CT])
        g_ms = sb("g_ms", [P, CT])
        g_shift = sb("g_shift", [P, CT])
        ident = cst[:, 0, :]
        gmat = cst[:, 1, :]

        ps_s = ctx.enter_context(nc.psum_tensor("ps_s", [P, 4, HALF], F32))
        ps_t = ctx.enter_context(nc.psum_tensor("ps_t", [P, 2, HALF], F32))
        ps_pv = ctx.enter_context(nc.psum_tensor("ps_pv", [P, HALF], F32))
        ps_qk = ctx.enter_context(nc.psum_tensor("ps_qk", [P, HALF], F32))

        v_view = va[:, 1:CT + 1, :].rearrange("p r (h t c) -> p (r h) t c", h=2, t=QT)
        a_view = va[:, 0:CT, :].rearrange("p r (w t) -> p r w t", w=2)

        s_const = sem("s_const")
        s_par = sem("s_par")
        s_gnpar = sem("s_gnpar")
        s_half = sem("s_half")
        s_qkbias = sem("s_qkbias")
        s_qkscale = sem("s_qkscale")
        s_qkshift = sem("s_qkshift")
        s_raw = [sem(f"s_raw{i}") for i in range(RAW)]
        s_whigh = sem("s_whigh")
        s_wlow = sem("s_wlow")
        s_x = [sem(f"s_x{i}") for i in range(CT)]
        s_stats = sem("s_stats")
        s_gmean = sem("s_gmean")
        s_spread = sem("s_spread")
        s_gspread = sem("s_gspread")
        s_gvar = sem("s_gvar")
        s_shift = sem("s_shift")
        s_applied = sem("s_applied")
        s_xhigh = sem("s_xhigh")
        s_xlow = sem("s_xlow")
        s_dve = sem("s_dve")
        s_pool = sem("s_pool")
        s_qk = sem("s_qk")
        s_qkfull = sem("s_qkfull")
        s_qkhigh = sem("s_qkhigh")
        s_qklow = sem("s_qklow")
        s_kput = [[sem(f"s_kput{s}{k}") for k in range(2)] for s in range(2)]
        s_qput = [[sem(f"s_qput{s}{k}") for k in range(2)] for s in range(2)]
        s_v = sem("s_v")
        s_vhigh = sem("s_vhigh")
        s_vlow = sem("s_vlow")
        s_score = sem("s_score")
        s_max = sem("s_max")
        s_exp = sem("s_exp")
        s_inv = sem("s_inv")
        s_norm = sem("s_norm")
        s_trans = sem("s_trans")
        s_phigh = sem("s_phigh")
        s_plow = sem("s_plow")
        s_pv = sem("s_pv")
        s_ocopy = sem("s_ocopy")
        s_osum = sem("s_osum")
        s_ohigh = sem("s_ohigh")
        s_o = sem("s_o")
        s_partial = sem("s_partial")
        s_joined = sem("s_joined")
        s_proj = sem("s_proj")
        s_y = sem("s_y")
        s_res = [sem(f"s_res{j}") for j in range(NP)]
        s_out = [sem(f"s_out{j}") for j in range(NP)]

        def image(t, b):
            return t[b].rearrange("(ct p) n -> p ct n", p=P)

        def res_tile(j):
            o, k = j % CT, j // CT
            return res[:, j, :] if j < RES else xin[:, o, HALF * k:HALF * k + HALF]

        def out_bank(j):
            return ps_qk[:, :] if j == 1 else ps_s[:, max(j, 1) % 4, :]

        raw_ahead = [len([i for i in range(FIRST_NEXT, UNITS) if i % RAW == s]) for s in range(RAW)]

        def unit_parts(i):
            kind, at = USES[i]
            return wqk[:, at % 2] if kind == "qk" else wvp[:, at]

        def units_done(n, i):
            return UNITS * n + AHEAD + i + 1

        def qk_piece(g):
            i, lo = 2 + (g + 2) // 4, PIECE * ((g + 2) % 4)
            return (i, lo, lo + PIECE) if i < 2 * HEADS else None

        def exp_early(g):
            return 6 <= g < G and g % 4 == 2

        def wait_apart(eng, *waits):
            for _, value in waits:
                if not isinstance(value, int):
                    eng.compute_val(value)
            eng.wait_ge(s_const, 16)
            for semaphore, value in waits:
                eng.wait_ge(semaphore, value)

        block = ctx.enter_context(nc.Block())

        @block.sync
        def _(sp):
            def put_qk(n, h, k):
                sp.wait_ge(s_qklow, 2 * HEADS * n + 2 * h + k + 1)
                s, cols = h % 2, slice(HALF * k, HALF * k + HALF)
                q_rows, k_rows = slice(0, CH), slice(CH, P)
                for to, of in ((k_lh[0:CH, s, cols], qk_part[k_rows, 1, :]),
                               (k_lh[CH:P, s, cols], qk_part[k_rows, 0, :])):
                    sp.dma_start(to.bitcast(F32), of.bitcast(F32)).then_inc(s_kput[s][k], 16)
                for to, of in ((q_parts[0:CH, :, s, cols], qk_part[q_rows, :, :]),
                               (q_parts[CH:P, 0, s, cols], qk_part[q_rows, 1, :]),
                               (q_parts[CH:P, 1, s, cols], qk_part[q_rows, 0, :])):
                    sp.dma_start(to.bitcast(F32), of.bitcast(F32)).then_inc(s_qput[s][k], 16)

            def load_unit(n, i, layer):
                kind, at = USES[i]
                unit = {"qk": at, "v": HEADS + at, "out": HEADS + CT + at}[kind]
                sp.dma_start(raw[:, i % RAW, :], weights[layer, unit]).then_inc(s_raw[i % RAW], 16)

            def next_unit(n, i):
                wait_apart(sp, (s_wlow, units_done(n, i - RAW)))
                load_unit(n, i, n // B if i < FIRST_NEXT else (n + 1) // B % LAYERS)

            for ct in range(CT):
                sp.dma_start(xin[:, ct, :], image(x, 0)[:, ct, :]).then_inc(s_x[ct], 16)
                if ct == 0:
                    sp.dma_start(cst[:, :, :], consts).then_inc(s_const, 16)
                    sp.dma_start(gn_par[:, :], gn_params[0]).then_inc(s_gnpar, 16)
            sp.dma_start(qk_bias[:, :], qk_params[0]).then_inc(s_qkbias, 16)
            for i in range(FIRST_NEXT, UNITS - 1):
                load_unit(-1, i, 0)
            sp.dma_start(par[:, :], params[0]).then_inc(s_par, 16)
            sp.wait_ge(s_wlow, 1)
            load_unit(-1, UNITS - 1, 0)

            with sp.Fori(0, N) as n:
                nxt = (n + 1) // B % LAYERS

                def load_res(j):
                    o, k = j % CT, j // CT
                    src = slice(k * HALF, (k + 1) * HALF)
                    with sp.If(n < B):
                        sp.dma_start(res_tile(j), image(x, n % B)[:, o, src]).then_inc(s_res[j], 16)
                    with sp.Else():
                        sp.dma_start(res_tile(j), image(hidden, n % B)[:, o, src]).then_inc(s_res[j], 16)

                def store_res(j):
                    o, k = j % CT, j // CT
                    dst = slice(k * HALF, (k + 1) * HALF)
                    wait_apart(sp, (s_y, NP * n + j + 1))
                    with sp.If(n < B):
                        sp.dma_start(image(hidden, n % B)[:, o, dst], res_tile(j)).then_inc(s_out[j], 16)
                    with sp.Else():
                        sp.dma_start(image(out, n % B)[:, o, dst], res_tile(j)).then_inc(s_out[j], 16)

                wait_apart(sp, (s_xlow, 2 * CT * (n + 1)))
                with sp.If(n + 1 < B):
                    for ct in range(CT):
                        sp.dma_start(xin[:, ct, :], image(x, (n + 1) % B)[:, ct, :]).then_inc(s_x[ct], 16)
                with sp.Else():
                    for ct in range(CT):
                        sp.dma_start(xin[:, ct, :], image(hidden, (n + 1) % B)[:, ct, :]).then_inc(s_x[ct], 16)
                sp.dma_start(gn_par[:, :], gn_params[nxt]).then_inc(s_gnpar, 16)
                put_qk(n, 0, 0)
                for i in range(RAW):
                    next_unit(n, i)
                put_qk(n, 0, 1)
                for j in range(RES):
                    load_res(j)
                next_unit(n, RAW)
                for i in range(2, 2 * HEADS):
                    put_qk(n, i // 2, i % 2)
                    if 4 * i - 6 in SPLIT_AT:
                        next_unit(n, SPLIT_AT[4 * i - 6] + RAW)
                sp.dma_start(qk_bias[:, :], qk_params[nxt]).then_inc(s_qkbias, 16)
                wait_apart(sp, (s_xlow, 2 * CT * (n + 2)))
                for j in range(RES, NP):
                    load_res(j)
                for j in range(NP):
                    store_res(j)
                sp.dma_start(par[:, :], params[nxt]).then_inc(s_par, 16)
                wait_apart(sp, *((s_out[j], 16 * (n + 1)) for j in range(NP)))
            sp.wait_ge(s_par, 16 * (N + 1))
            sp.wait_ge(s_qkbias, 16 * (N + 1))
            for ct in range(CT):
                sp.wait_ge(s_x[ct], 16 * (N + 1))

        @block.gpsimd
        def _(pool):
            PER_GN = 3

            def gn_coeffs(m):
                c = PER_GN * m
                pool.wait_ge(s_gnpar, 16 * m + 16)
                pool.wait_ge(s_gvar, m + 1)
                nc.gpsimd.tensor_tensor(g_rstd[:, :], g_var[:, :], minus_half[:, :], ALU.pow).then_inc(s_pool, 1)
                pool.wait_ge(s_pool, c + 1)
                nc.gpsimd.tensor_tensor(g_scale[:, :], g_rstd[:, :], gn_par[:, 0:CT], ALU.mult).then_inc(s_pool, 1)
                pool.wait_ge(s_pool, c + 2)
                nc.gpsimd.tensor_tensor(g_ms[:, :], g_mean[:, :], g_scale[:, :], ALU.mult).then_inc(s_pool, 1)
                pool.wait_ge(s_pool, c + 3)
                nc.gpsimd.tensor_tensor(g_shift[:, :], gn_par[:, CT:2 * CT], g_ms[:, :], ALU.subtract).then_inc(s_shift, 1)

            def gn_apply(m, ct):
                wait_apart(pool, (s_shift, m + 1))
                nc.gpsimd.tensor_scalar(xin[:, ct, :], xin[:, ct, :], g_scale[:, ct:ct + 1], g_shift[:, ct:ct + 1],
                                        ALU.mult, ALU.add).then_inc(s_applied, 1)

            def gn_low(m, i):
                ct, cols = i // 2, slice(HALF * (i % 2), HALF * (i % 2) + HALF)
                pool.wait_ge(s_xhigh, 2 * CT * m + i + 1)
                nc.gpsimd.tensor_tensor(xn[:, 1, ct, cols], xin[:, ct, cols], xn[:, 0, ct, cols].bitcast(F32),
                                        ALU.subtract).then_inc(s_xlow, 1)

            def weight_low(n, i):
                pool.wait_ge(s_whigh, units_done(n, i))
                parts = unit_parts(i)
                nc.gpsimd.tensor_tensor(parts[:, 1, :], raw[:, i % RAW, :], parts[:, 0, :].bitcast(F32),
                                        ALU.subtract).then_inc(s_wlow, 1)

            pool.wait_ge(s_half, 1)
            weight_low(-1, FIRST_NEXT)
            gn_coeffs(0)
            for ct in range(CT):
                gn_apply(0, ct)
            for i in range(FIRST_V, UNITS):
                weight_low(-1, i)

            with pool.Fori(0, N) as n:
                def normalise(g):
                    s = g % LAG
                    wait_apart(pool, (s_inv, G * n + g + 1))
                    nc.gpsimd.tensor_scalar(probs[:, s, :], probs[:, s, :], row_inv[:, g % 4:g % 4 + 1], 1.0,
                                            ALU.mult, ALU.mult).then_inc(s_norm, 1)

                def qk_low(i):
                    wait_apart(pool, (s_qkhigh, 16 * n + i + 1))
                    nc.gpsimd.tensor_tensor(qk_part[:, 1, :], qk_full[:, :], qk_part[:, 0, :].bitcast(F32),
                                            ALU.subtract).then_inc(s_qklow, 1)

                def split_out(k, before, count):
                    h = k // 2
                    r = slice(CH * (h % 2), CH * (h % 2) + CH)
                    cols = slice(HALF * (k % 2), HALF * (k % 2) + HALF)
                    wait_apart(pool, (before, count), (s_osum, NG * n + k + 1))
                    nc.gpsimd.tensor_scalar(a_view[r, h // 2, 0, cols], head_out[r, 0, :], 1.0, 1.0,
                                            ALU.mult, ALU.mult).then_inc(s_ohigh, 1)
                    pool.wait_ge(s_ohigh, NG * n + k + 1)
                    nc.gpsimd.tensor_tensor(a_view[r, h // 2, 1, cols], head_out[r, 0, :],
                                            a_view[r, h // 2, 0, cols].bitcast(F32), ALU.subtract).then_inc(s_o, 1)
                    wait_apart(pool, (s_o, NG * n + k + 1))

                qk_low(0)
                qk_low(1)
                weight_low(n, 0)
                gn_coeffs(n + 1)
                for g in range(G + LAG):
                    if qk_piece(g - 1) and qk_piece(g - 1)[2] == 3 * CT:
                        qk_low(qk_piece(g - 1)[0])
                    if 1 <= g <= G:
                        normalise(g - 1)
                    if g in PUT_AT:
                        split_out(PUT_AT[g], s_norm, G * n + g)
                    if g in SPLIT_AT:
                        weight_low(n, SPLIT_AT[g])
                    if g in APPLY_AT:
                        gn_apply(n + 1, APPLY_AT[g])
                    if g in LOW_AT:
                        gn_low(n + 1, LOW_AT[g])
                for i in range(len(LOW_AT), 2 * CT):
                    gn_low(n + 1, i)
                split_out(NG - 1, s_xlow, 2 * CT * (n + 2))
                for i in range(FIRST_V, UNITS):
                    weight_low(n, i)

        @block.scalar
        def _(act):
            def gn_high(m, i):
                ct, cols = i // 2, slice(HALF * (i % 2), HALF * (i % 2) + HALF)
                act.wait_ge(s_applied, CT * m + ct + 1)
                nc.scalar.activation(xn[:, 0, ct, cols], xin[:, ct, cols], ACT.Copy).then_inc(s_xhigh, 1)

            def weight_high(n, i):
                s = i % RAW
                act.wait_ge(s_raw[s], 16 * (UNITS // RAW * n + raw_ahead[s] + i // RAW + 1))
                nc.scalar.activation(unit_parts(i)[:, 0, :], raw[:, s, :], ACT.Copy).then_inc(s_whigh, 1)

            for i in range(FIRST_NEXT, UNITS - 1):
                weight_high(-1, i)
            for i in range(2 * CT):
                gn_high(0, i)
            weight_high(-1, UNITS - 1)

            with act.Fori(0, N) as n:
                def qk_out(i):
                    act.wait_ge(s_qk, 16 * n + i + 1)
                    if i == 0:
                        act.wait_ge(s_qkshift, n + 1)
                    else:
                        act.wait_ge(s_qklow, 16 * n + i)
                    nc.scalar.activation(qk_full[:, :], ps_qk[:, :], ACT.Identity, bias=qk_shift[:, i // 2:i // 2 + 1],
                                         scale=qk_scale[:, :]).then_inc(s_qkfull, 1)

                def qk_high(i):
                    act.wait_ge(s_qkfull, 16 * n + i + 1)
                    if i:
                        s, k, count = (i - 1) // 2 % 2, (i - 1) % 2, HEADS // 2 * n + (i - 1) // 4 + 1
                        act.wait_ge(s_kput[s][k], K_PUTS * count)
                        act.wait_ge(s_qput[s][k], Q_PUTS * count)
                    nc.scalar.activation(qk_part[:, 0, :], qk_full[:, :], ACT.Copy).then_inc(s_qkhigh, 1)

                def v_high(t):
                    act.wait_ge(s_v, QT * n + t + 1)
                    nc.scalar.activation(v_view[:, :, t, 0:CH], ps_s[:, t % 4, :].rearrange("p (h c) -> p h c", h=HEADS),
                                         ACT.Copy).then_inc(s_vhigh, 1)

                def exp(g):
                    b = 2 * (g % 2)
                    act.wait_ge(s_max, G * n + g + 1)
                    nc.scalar.activation(probs[:, g % LAG, :].rearrange("p (b n) -> p b n", b=2), ps_s[:, b:b + 2, :],
                                         ACT.Exp, bias=neg_max[:, g % 4:g % 4 + 1],
                                         accum_out=row_sum[:, g % 4:g % 4 + 1]).then_inc(s_exp, 1)

                def probs_high(g, b):
                    act.wait_ge(s_trans, 2 * G * n + 2 * g + b + 1)
                    if g % 4 == 0 and b == 0 and g:
                        act.wait_ge(s_pv, NG * n + g // 4)
                    q = P * (g % 4)
                    nc.scalar.activation(probs_t[:, 0, 4 * b:4 * b + 4, q:q + P],
                                         ps_t[:, b, :].rearrange("p (k q) -> p k q", k=4), ACT.Copy).then_inc(s_phigh, 1)

                def copy_out(k):
                    act.wait_ge(s_pv, NG * n + k + 1)
                    if k:
                        act.wait_ge(s_o, NG * n + k)
                    nc.scalar.activation(head_out[0:CH, 0, :], ps_pv[0:CH, :], ACT.Identity,
                                         bias=par[0:CH, k // 2:k // 2 + 1])
                    nc.scalar.activation(head_out[0:CH, 1, :], ps_pv[CH:P, :], ACT.Copy).then_inc(s_ocopy, 1)

                qk_out(0)
                qk_high(0)
                v_high(0)
                v_high(1)
                qk_out(1)
                qk_high(1)
                for t in range(2, QT):
                    v_high(t)
                    if t == 4:
                        weight_high(n, 0)
                for g in range(G + LAG):
                    if g >= LAG:
                        probs_high(g - LAG, 0)
                        probs_high(g - LAG, 1)
                    if qk_piece(g - 1) and qk_piece(g - 1)[2] == 3 * CT:
                        qk_high(qk_piece(g - 1)[0])
                    if 1 <= g <= G and not exp_early(g - 1):
                        exp(g - 1)
                    if qk_piece(g) and qk_piece(g)[2] == 3 * CT:
                        qk_out(qk_piece(g)[0])
                    if g in COPY_AT:
                        copy_out(COPY_AT[g])
                    if exp_early(g):
                        exp(g)
                    if g in SPLIT_AT:
                        weight_high(n, SPLIT_AT[g])
                    for i in HIGH_AT.get(g, ()):
                        gn_high(n + 1, i)
                copy_out(NG - 1)
                for ct in range(CT):
                    act.wait_ge(s_proj, NP * n + CT + ct + 1)
                    weight_high(n, FIRST_V + ct)

        @block.vector
        def _(dve):
            PER_GN = 4

            def gn_stats(m, ct):
                dve.wait_ge(s_x[ct], 16 * m + 16)
                for k in range(2):
                    last = nc.vector.bn_stats(bn_part[:, ct, k, :], xin[:, ct, HALF * k:HALF * k + HALF])
                if ct == CT - 1:
                    last.then_inc(s_dve, 1)
                    wait_apart(dve, (s_dve, PER_GN * m + 1))
                    for i in range(CT):
                        last = nc.vector.bn_aggr(bn_mv[:, i, :], bn_part[:, i, :, :].rearrange("p k s -> p (k s)"))
                    last.then_inc(s_stats, 1)

            def gn_spread(m):
                c = PER_GN * m
                dve.wait_ge(s_gmean, m + 1)
                nc.vector.tensor_copy(g_mean[:, :], ps_pv[:, 0:CT]).then_inc(s_dve, 1)
                dve.wait_ge(s_dve, c + 2)
                nc.vector.tensor_tensor(g_dev[:, :], bn_mv[:, :, 0], g_mean[:, :], ALU.subtract).then_inc(s_dve, 1)
                dve.wait_ge(s_dve, c + 3)
                nc.vector.tensor_tensor(g_sq[:, :], g_dev[:, :], g_dev[:, :], ALU.mult).then_inc(s_dve, 1)
                dve.wait_ge(s_dve, c + 4)
                nc.vector.tensor_tensor(g_spread[:, :], g_sq[:, :], bn_mv[:, :, 1], ALU.add).then_inc(s_spread, 1)

            def gn_var(m):
                dve.wait_ge(s_gspread, m + 1)
                nc.vector.tensor_scalar(g_var[:, :], ps_pv[:, CT:2 * CT], EPS, None, ALU.add).then_inc(s_gvar, 1)

            def scale_biases(m):
                dve.wait_ge(s_qkbias, 16 * m + 16)
                nc.vector.tensor_scalar(qk_shift[:, :], qk_bias[:, :], qk_scale[:, :], None, ALU.mult).then_inc(s_qkshift, 1)

            nc.vector.memset(minus_half[:, :], -0.5).then_inc(s_half, 1)
            nc.vector.memset(qk_scale[0:CH, :], SCALE).then_inc(s_qkscale, 1)
            nc.vector.memset(qk_scale[CH:P, :], 1.0).then_inc(s_qkscale, 1)
            for ct in range(CT):
                gn_stats(0, ct)
            gn_spread(0)
            gn_var(0)
            dve.wait_ge(s_qkscale, 2)
            scale_biases(0)
            for ct in range(CT):
                for k in range(2):
                    dve.wait_ge(s_xhigh, 2 * ct + k + 1)
                    cols = slice(HALF * k, HALF * k + HALF)
                    nc.vector.tensor_tensor(xn[:, 1, ct, cols], xin[:, ct, cols], xn[:, 0, ct, cols].bitcast(F32),
                                            ALU.subtract).then_inc(s_xlow, 1)

            with dve.Fori(0, N) as n:
                def v_low(t):
                    dve.wait_ge(s_vhigh, QT * n + t + 1)
                    nc.vector.tensor_tensor(v_view[:, :, t, CH:P], ps_s[:, t % 4, :].rearrange("p (h c) -> p h c", h=HEADS),
                                            v_view[:, :, t, 0:CH].bitcast(F32), ALU.subtract).then_inc(s_vlow, 1)

                def row_max(g):
                    b = 2 * (g % 2)
                    dve.wait_ge(s_score, G * n + g + 1)
                    nc.vector.reduce_max(neg_max[:, g % 4:g % 4 + 1], ps_s[:, b:b + 2, :], AX.XY,
                                         negate=True).then_inc(s_max, 1)

                def row_inverse(g):
                    dve.wait_ge(s_exp, G * n + g + 1)
                    nc.vector.reciprocal(row_inv[:, g % 4:g % 4 + 1], row_sum[:, g % 4:g % 4 + 1]).then_inc(s_inv, 1)

                def probs_low(g, b):
                    dve.wait_ge(s_phigh, 2 * G * n + 2 * g + b + 1)
                    q = P * (g % 4)
                    nc.vector.tensor_tensor(probs_t[:, 1, 4 * b:4 * b + 4, q:q + P],
                                            ps_t[:, b, :].rearrange("p (k q) -> p k q", k=4),
                                            probs_t[:, 0, 4 * b:4 * b + 4, q:q + P].bitcast(F32),
                                            ALU.subtract).then_inc(s_plow, 1)

                def out_sum(k):
                    h = k // 2
                    r = slice(CH * (h % 2), CH * (h % 2) + CH)
                    dve.wait_ge(s_ocopy, NG * n + k + 1)
                    nc.vector.tensor_tensor(head_out[r, 0, :], head_out[0:CH, 0, :], head_out[0:CH, 1, :],
                                            ALU.add).then_inc(s_osum, 1)

                def add_residual(j):
                    o = j % CT
                    dve.wait_ge(s_proj, NP * n + j + 1)
                    dve.wait_ge(s_res[j], 16 * (n + 1))
                    nc.vector.scalar_tensor_tensor(res_tile(j), out_bank(j), par[:, HEADS + o:HEADS + o + 1],
                                                   res_tile(j), ALU.add, ALU.add).then_inc(s_y, 1)

                for t in range(QT):
                    v_low(t)
                    if 1 <= t < 1 + CT:
                        gn_stats(n + 1, t - 1)
                    if t == QT - 2:
                        gn_spread(n + 1)
                gn_var(n + 1)
                for g in range(G + LAG):
                    if g >= LAG:
                        probs_low(g - LAG, 0)
                        probs_low(g - LAG, 1)
                    if g in SUM_AT:
                        out_sum(SUM_AT[g])
                    if 1 <= g <= G and not exp_early(g - 1):
                        row_inverse(g - 1)
                    if g < G:
                        row_max(g)
                    if exp_early(g):
                        row_inverse(g)
                    if g == PARTIAL_AT:
                        dve.wait_ge(s_partial, n + 1)
                        dve.wait_ge(s_res[0], 16 * (n + 1))
                        nc.vector.tensor_tensor(res_tile(0), ps_qk[:, :], res_tile(0), ALU.add).then_inc(s_joined, 1)
                    if g == BIASES_AT:
                        dve.wait_ge(s_qkfull, 16 * n + 16)
                        scale_biases(n + 1)
                add_residual(0)
                out_sum(NG - 1)
                for j in range(1, NP):
                    add_residual(j)

        @block.tensor
        def _(pe):
            def group_mean(m):
                pe.wait_ge(s_stats, m + 1)
                nc.tensor.matmul(ps_pv[:, 0:CT], gmat, bn_mv[:, :, 0], start=True, stop=True).then_inc(s_gmean, 1)

            def group_spread(m):
                pe.wait_ge(s_spread, m + 1)
                nc.tensor.matmul(ps_pv[:, CT:2 * CT], gmat, g_spread[:, :], start=True, stop=True).then_inc(s_gspread, 1)

            pe.wait_ge(s_const, 16)
            group_mean(0)
            group_spread(0)

            with pe.Fori(0, N) as n:
                def project_qk(i, lo, hi):
                    h, k = i // 2, i % 2
                    if k == 0 and lo == 0:
                        pe.wait_ge(s_wlow, units_done(n, USES.index(("qk", h)) if h else FIRST_NEXT - UNITS))
                    if lo == 0 and i > 0:
                        pe.wait_ge(s_qkfull, 16 * n + i)
                    for j in range(lo, hi):
                        w, v = TERMS[j // CT]
                        last = nc.tensor.matmul(ps_qk[:, :], wqk[:, h % 2, w, P * (j % CT):P * (j % CT) + P],
                                                xn[:, v, j % CT, HALF * k:HALF * k + HALF],
                                                start=j == 0, stop=j == 3 * CT - 1)
                    if hi == 3 * CT:
                        last.then_inc(s_qk, 1)

                def project_v(t):
                    if t == 3:
                        pe.wait_ge(s_par, 16 * n + 16)
                    if t >= 4:
                        pe.wait_ge(s_vlow, QT * n + t - 3)
                    if t == 0:
                        pe.wait_ge(s_wlow, units_done(n, -1))
                    for j in range(3 * CT):
                        w, v = TERMS[j // CT]
                        last = nc.tensor.matmul(ps_s[:, t % 4, :], xn[:, v, j % CT, P * t:P * t + P], wvp[:, j % CT, w, :],
                                                start=j == 0, stop=j == 3 * CT - 1)
                    last.then_inc(s_v, 1)

                def scores(g):
                    h, qt, b = g // QT, g % QT, 2 * (g % 2)
                    s = h % 2
                    if qt == 0:
                        for k in range(2):
                            pe.wait_ge(s_kput[s][k], K_PUTS * (HEADS // 2 * n + h // 2 + 1))
                    if qt in (0, 4):
                        pe.wait_ge(s_qput[s][qt // 4], Q_PUTS * (HEADS // 2 * n + h // 2 + 1))
                    if g < 2:
                        pe.wait_ge(s_vlow, QT * n + 6 + 2 * g)
                    else:
                        pe.wait_ge(s_exp, G * n + g - 1)
                    for w in range(2):
                        for k in range(2):
                            last = nc.tensor.matmul(ps_s[:, b + k, :], q_parts[:, w, s, P * qt:P * qt + P],
                                                    k_lh[:, s, HALF * k:HALF * k + HALF], start=w == 0, stop=w == 1)
                    last.then_inc(s_score, 1)

                def transpose(g):
                    pe.wait_ge(s_norm, G * n + g + 1)
                    for b in range(2):
                        if g:
                            pe.wait_ge(s_plow, 2 * G * n + 2 * g + b - 1)
                        for k in range(4):
                            c = 4 * b + k
                            last = nc.tensor.transpose(ps_t[:, b, P * k:P * k + P], probs[:, g % LAG, P * c:P * c + P], ident)
                        last.then_inc(s_trans, 1)

                def probs_v(k):
                    h = k // 2
                    if k:
                        pe.wait_ge(s_ocopy, NG * n + k)
                    else:
                        pe.wait_ge(s_vlow, QT * n + QT)
                        pe.wait_ge(s_gvar, n + 2)
                    for b in range(2):
                        for w, written in enumerate((s_phigh, s_plow)):
                            pe.wait_ge(written, 2 * G * n + 8 * k + 7 + b)
                            for kt in range(4 * b, 4 * b + 4):
                                last = nc.tensor.matmul(ps_pv[:, :], v_view[:, h, kt, :], probs_t[:, w, kt, :],
                                                        start=kt == 0 and w == 0, stop=kt == QT - 1 and w == 1)
                    last.then_inc(s_pv, 1)

                early, last = 3 * (CT - 1), 3 * CT

                def project_out(j, lo=0, hi=3 * CT):
                    o, k = j % CT, j // CT
                    bank = ps_qk[:, :] if j == 0 and lo < early else out_bank(j)
                    firsts, lasts = ((0, early), (early - 1, last - 1)) if j == 0 else ((0,), (last - 1,))
                    if lo == 0:
                        if j == 0:
                            pe.wait_ge(s_qkfull, 16 * n + 16)
                        if j == 1:
                            pe.wait_ge(s_joined, n + 1)
                        if j == 4:
                            pe.wait_ge(s_exp, G * n + G - 1)
                        if j == 2:
                            pe.wait_ge(s_exp, G * n + G)
                        if j > 4:
                            pe.wait_ge(s_y, NP * n + (1 if j == 5 else j - 3))
                        if j < 4:
                            pe.wait_ge(s_wlow, units_done(n, USES.index(("out", o))))
                    for i in range(lo, hi):
                        ct, (w, v) = i // 3, TERMS[i % 3]
                        if j < 2 and i % 3 == 0 and ct < CT - 1:
                            pe.wait_ge(s_o, NG * n + 4 * ct + 4)
                        if i == early:
                            pe.wait_ge(s_o, NG * n + NG - 1 + k)
                        mm = nc.tensor.matmul(bank, wvp[:, o, w, P * ct:P * ct + P],
                                              a_view[:, ct, v, HALF * k:HALF * k + HALF], start=i in firsts, stop=i in lasts)
                    if j == 0 and hi == early:
                        mm.then_inc(s_partial, 1)
                    if hi == last:
                        mm.then_inc(s_proj, 1)

                pe.wait_ge(s_xlow, 2 * CT * (n + 1))
                project_qk(0, 0, 3 * CT)
                project_v(0)
                project_v(1)
                project_qk(1, 0, 3 * CT)
                for t in range(2, QT):
                    if t == QT - 1:
                        group_mean(n + 1)
                    project_v(t)
                group_spread(n + 1)
                for g in range(G + LAG):
                    if g >= LAG:
                        transpose(g - LAG)
                    if g < G:
                        scores(g)
                    if g == 0:
                        project_qk(*qk_piece(-2))
                        project_qk(*qk_piece(-1))
                    if qk_piece(g):
                        project_qk(*qk_piece(g))
                    if g in OUT_PIECE_AT:
                        j, ct = OUT_PIECE_AT[g]
                        project_out(j, PIECE * ct, PIECE * ct + PIECE)
                    if g >= G:
                        project_out((4, 2, 3)[g - G], 0, early)
                    if g >= 6 and g % 4 == 2:
                        probs_v((g - 6) // 4)
                for j in range(4):
                    project_out(j, early, last)
                project_out(5, 0, early)
                project_out(4, early, last)
                project_out(5, early, last)
                for j in range(6, NP):
                    project_out(j)
                pe.wait_ge(s_y, NP * n + NP - 1)


def kernel(x, L0_conv_norm_w, L0_conv_norm_b, L0_conv_qkv_w, L0_conv_qkv_b, L0_conv_proj_w, L0_conv_proj_b,
           L1_conv_gn_scale, L1_conv_gn_bias, L1_conv_wq, L1_conv_bq, L1_conv_wk, L1_conv_bk, L1_conv_wv, L1_conv_bv,
           L1_conv_wp, L1_conv_bp):
    import numpy as np
    import concourse.bacc as bacc
    from concourse.bass_utils import run_bass_kernel_spmd

    w0 = np.asarray(L0_conv_qkv_w).reshape(HEADS, 3, CH, C)
    b0 = np.asarray(L0_conv_qkv_b).reshape(HEADS, 3, CH)
    layers = [
        (w0[:, 0], w0[:, 1], w0[:, 2], L0_conv_proj_w, b0[:, 0], b0[:, 1], b0[:, 2], L0_conv_proj_b,
         L0_conv_norm_w, L0_conv_norm_b),
        tuple(np.asarray(a).reshape(HEADS, CH, C) for a in (L1_conv_wq, L1_conv_wk, L1_conv_wv)) + (L1_conv_wp,)
        + tuple(np.asarray(a).reshape(HEADS, CH) for a in (L1_conv_bq, L1_conv_bk, L1_conv_bv)) + (L1_conv_bp,
         L1_conv_gn_scale, L1_conv_gn_bias),
    ]
    weights, qk_params, params, gn_params = [], [], [], []
    for wq, wk, wv, wp, bq, bk, bv, bp, gw, gb in layers:
        qk = np.concatenate([wq, wk], axis=1).reshape(HEADS, P, CT, P).transpose(0, 3, 2, 1).reshape(HEADS, P, HALF)
        v = np.asarray(wv).reshape(C, CT, P).transpose(1, 2, 0)
        p = np.asarray(wp).reshape(CT, P, CT, P).transpose(0, 3, 2, 1).reshape(CT, P, HALF)
        weights.append(np.concatenate([qk, v, p], axis=0))
        qk_params.append(np.concatenate([bq, bk], axis=1).T)
        par = np.zeros((P, HEADS + CT), np.float32)
        par[0:CH, 0:HEADS] = np.asarray(bv).T
        par[:, HEADS:] = np.asarray(bp).reshape(CT, P).T
        params.append(par)
        gn_params.append(np.concatenate([np.asarray(gw).reshape(CT, P).T, np.asarray(gb).reshape(CT, P).T], axis=1))
    consts = np.stack([np.eye(P), np.kron(np.eye(P // GROUP), np.full((GROUP, GROUP), 1.0 / GROUP))], axis=1)

    arrays = {
        "x": np.ascontiguousarray(np.asarray(x).reshape(B, C, T)),
        "weights": np.ascontiguousarray(np.stack(weights)),
        "qk_params": np.ascontiguousarray(np.stack(qk_params)),
        "params": np.ascontiguousarray(np.stack(params)),
        "gn_params": np.ascontiguousarray(np.stack(gn_params)),
        "consts": np.ascontiguousarray(consts.astype(np.float32)),
    }
    nc = bacc.Bacc("TRN2", target_bir_lowering=False, num_devices=1)
    ins = [nc.dram_tensor(name, a.shape, F32, kind="ExternalInput").ap() for name, a in arrays.items()]
    hidden = nc.dram_tensor("hidden", (B, C, T), F32, kind="Internal").ap()
    out = nc.dram_tensor("out", (B, C, T), F32, kind="ExternalOutput").ap()
    attention_blocks(nc, *ins, hidden, out)
    r = run_bass_kernel_spmd(nc, [arrays], core_ids=[0])
    return r.results[0]["out"].reshape(B, C, 32, 32)
```
